# Optimizing a Trainium2 kernel written in Bass

```python
import numpy as np
import jax
import jax.numpy as jnp

def _softmax(x, axis=-1):
    return jax.nn.softmax(x, axis=axis)
def _gelu(x):
    return jax.nn.gelu(x, approximate=True)
def _silu(x):
    return jax.nn.silu(x)
def _sigmoid(x):
    return jax.nn.sigmoid(x)
def _layernorm(x, axis=-1, eps=1e-5):
    m = jnp.mean(x, axis=axis, keepdims=True)
    v = jnp.var(x, axis=axis, keepdims=True)
    return (x - m) / jnp.sqrt(v + eps)
def _scatter_add(tgt, idx, src, axis=0):
    return tgt.at[idx].add(src)
def _segment_sum(src, seg, n):
    return jax.ops.segment_sum(src, seg, n)

kernel_name = 'mk_adj_resnorm_d2_adj_512_a51daa'

def setup_inputs(seed: int = 0):
    np.random.seed(seed)
    _w = jnp.asarray
    def _rec_inputs():
        import jax
        import jax.numpy as jnp
        _gk = jax.random.key(seed)
        x = -0.0001117 + 0.9999 * jax.random.normal(jax.random.fold_in(_gk, 1), (32, 512, 512), jnp.float32)
        _a = jax.random.bernoulli(jax.random.fold_in(_gk, 2), 0.015625, (512, 512))
        _a = jnp.logical_or(_a, jnp.swapaxes(_a, -1, -2))
        _a = jnp.logical_or(_a, jnp.eye(512, dtype=bool))
        adj = _a.astype(jnp.int32)
        return x, adj
    x, adj = _rec_inputs()
    def _L0_gnn_setup():
        import jax, jax.numpy as jnp
        import numpy as np
        B, N, F, F1 = (1024, 75, 512, 256)
        NEG = -1000000000.0
        ALPHA = 0.2
        key = jax.random.key(seed)
        k1, k2, k3, k4 = jax.random.split(key, 4)
        X = jax.random.normal(k1, (B, N, F), dtype=jnp.float32)
        A = jax.random.randint(k2, (N, N), 0, 2, dtype=jnp.int32)
        W = jax.random.normal(k3, (F, F1), dtype=jnp.float32) * (1.0 / np.sqrt(F))
        a = jax.random.normal(k4, (2, F1, 1), dtype=jnp.float32) * (1.0 / np.sqrt(F1))
        return {'X': X, 'A': A, 'W': W, 'a': a}
    _L0_gnn_all = _L0_gnn_setup()
    _L0_gnn_in = {k: v for k, v in _L0_gnn_all.items() if k in ('W', 'a', )}
    del _L0_gnn_all

    def _L1_gnn_setup():
        import jax, jax.numpy as jnp
        import numpy as np
        D_MODEL = 512
        NUM_HEADS = 8
        D_HEAD = D_MODEL // NUM_HEADS
        B, N = (4, 2048)
        key = jax.random.key(seed)
        ks = jax.random.split(key, 10)
        s = 1.0 / np.sqrt(D_MODEL)
        inp = {'h': jax.random.normal(ks[0], (B, N, D_MODEL), dtype=jnp.float32), 'adj': jax.random.randint(ks[1], (N, N), 0, 2, dtype=jnp.int32), 'Wq': jax.random.uniform(ks[2], (D_MODEL, D_MODEL), jnp.float32, -s, s), 'bq': jax.random.uniform(ks[3], (D_MODEL,), jnp.float32, -s, s), 'Wk': jax.random.uniform(ks[4], (D_MODEL, D_MODEL), jnp.float32, -s, s), 'bk': jax.random.uniform(ks[5], (D_MODEL,), jnp.float32, -s, s), 'Wv': jax.random.uniform(ks[6], (D_MODEL, D_MODEL), jnp.float32, -s, s), 'bv': jax.random.uniform(ks[7], (D_MODEL,), jnp.float32, -s, s), 'Wo': jax.random.uniform(ks[8], (D_MODEL, D_MODEL), jnp.float32, -s, s), 'bo': jax.random.uniform(ks[9], (D_MODEL,), jnp.float32, -s, s)}
        return inp
    _L1_gnn_all = _L1_gnn_setup()
    _L1_gnn_in = {k: v for k, v in _L1_gnn_all.items() if k in ('Wq', 'bq', 'Wk', 'bk', 'Wv', 'bv', 'Wo', 'bo', )}
    del _L1_gnn_all

    return {
        "x": x,
        "adj": adj,
        "L0_gnn_W": _L0_gnn_in["W"],
        "L0_gnn_a": _L0_gnn_in["a"],
        "L1_gnn_Wq": _L1_gnn_in["Wq"],
        "L1_gnn_bq": _L1_gnn_in["bq"],
        "L1_gnn_Wk": _L1_gnn_in["Wk"],
        "L1_gnn_bk": _L1_gnn_in["bk"],
        "L1_gnn_Wv": _L1_gnn_in["Wv"],
        "L1_gnn_bv": _L1_gnn_in["bv"],
        "L1_gnn_Wo": _L1_gnn_in["Wo"],
        "L1_gnn_bo": _L1_gnn_in["bo"],
    }

def reference(x, adj, L0_gnn_W, L0_gnn_a, L1_gnn_Wq, L1_gnn_bq, L1_gnn_Wk, L1_gnn_bk, L1_gnn_Wv, L1_gnn_bv, L1_gnn_Wo, L1_gnn_bo):
    import jax
    import jax.numpy as jnp
    def _L0_gnn_ref(X, A, W, a):
        import jax, jax.numpy as jnp
        import numpy as np
        B, N, F, F1 = (1024, 75, 512, 256)
        NEG = -1000000000.0
        ALPHA = 0.2
        h = jnp.einsum('bnf,fo->bno', X, W)
        att_self = jnp.einsum('bno,od->bnd', h, a[0])
        att_neigh = jnp.einsum('bno,od->bnd', h, a[1])
        e = att_self + jnp.swapaxes(att_neigh, 1, 2)
        e = jax.nn.leaky_relu(e, ALPHA)
        adj = A.astype(h.dtype)
        e = e + NEG * (1.0 - adj)[None, :, :]
        alpha = jax.nn.softmax(e, axis=-1)
        out = jnp.einsum('bij,bjo->bio', alpha, h)
        return jnp.concatenate([out, h], axis=-1)

    def _L1_gnn_ref(h, adj, Wq, bq, Wk, bk, Wv, bv, Wo, bo):
        import jax, jax.numpy as jnp
        import numpy as np
        D_MODEL = 512
        NUM_HEADS = 8
        D_HEAD = D_MODEL // NUM_HEADS
        B, N = (4, 2048)
        b, n, _ = h.shape

        def split_heads(x):
            return x.reshape(b, n, NUM_HEADS, D_HEAD).transpose(0, 2, 1, 3)
        q = split_heads(h @ Wq.T + bq)
        k = split_heads(h @ Wk.T + bk)
        v = split_heads(h @ Wv.T + bv)
        scale = 1.0 / np.sqrt(D_HEAD)
        scores = jnp.einsum('bhqd,bhkd->bhqk', q, k) * scale
        mask = (adj == 0)[None, None, :, :]
        scores = jnp.where(mask, -jnp.inf, scores)
        attn = jax.nn.softmax(scores, axis=-1)
        out = jnp.einsum('bhqk,bhkd->bhqd', attn, v)
        out = out.transpose(0, 2, 1, 3).reshape(b, n, D_MODEL)
        return out @ Wo.T + bo

    x = _layernorm(x + _L0_gnn_ref(x, adj, L0_gnn_W, L0_gnn_a), axis=-1)
    x = _layernorm(x + _L1_gnn_ref(x, adj, L1_gnn_Wq, L1_gnn_bq, L1_gnn_Wk, L1_gnn_bk, L1_gnn_Wv, L1_gnn_bv, L1_gnn_Wo, L1_gnn_bo), axis=-1)
    return x


_drawn_inputs = setup_inputs


def setup_inputs(seed=0):
    import zlib

    import numpy as np

    out = dict(_drawn_inputs(seed))
    spreads = {}
    factors = {'L1_gnn_bq': 48.391, 'L1_gnn_bk': 64.0, 'L1_gnn_bv': 3.894}
    for name, (base, spread) in spreads.items():
        noise = np.random.default_rng([zlib.crc32(name.encode()), seed]).standard_normal(out[name].shape)
        drawn = base * np.exp(spread * noise) if base else spread * noise
        out[name] = jnp.asarray(drawn.astype(out[name].dtype))
    for name, factor in factors.items():
        out[name] = (out[name] * factor).astype(out[name].dtype)
    return out
```

```python
from contextlib import ExitStack

import concourse.bass as bass
from concourse import mybir

ALU = mybir.AluOpType
ACT = mybir.ActivationFunctionType
F32 = mybir.dt.float32
F32R = mybir.dt.float32r
BF16 = mybir.dt.bfloat16
I32 = mybir.dt.int32

P = 128
HEADS = 8
EPS = 1e-5
LEAK = 0.2
NEG = -1.0e9
MASKED = -3.0e38
HUGE = 3.0e38
HI, LO = 0, 1
PARTS = ((HI, HI), (HI, LO), (LO, HI))

FIRST_LAYER = ["B0", "B1", "B2", "B3", "D0", "D1", "D2", "D3", "q0", "k0", "V0", "V1", "V2", "V3"]
ROUND = ["q1", "k1", "B0", "B1", "B2", "B3", "q2", "k2", "D0", "D1", "D2", "D3", "q3", "k3",
         "q0", "k0", "V0", "V1", "V2", "V3", "O0", "O1", "O2", "O3"]
LAST_ROUND = ["q1", "k1", "q2", "k2", "q3", "k3", "O0", "O1", "O2", "O3"]
TURNS = ["A0", "A1", "A2", "A3", "N", "C0", "C1", "C2", "C3", "E0", "E1", "E2", "E3"]
NEXT_ONLY = set("ABNCDEV") | {"nbm", "pre", "red", "aexp", "lst", "lrs", "lap", "bo"}

PLAN = {
    (0, 0): ["fin", "qk1"], (0, 1): ["evA1"], (0, 2): ["evB1"],
    (1, 0): ["A0"], (1, 1): ["A1", "B0"], (1, 2): ["A2", "B1"], (1, 3): ["A3", "B2"],
    (2, 0): ["B3", "qk2"], (2, 1): ["nbm", "N", "evA2"], (2, 2): ["evB2", "pre0", "pre1", "red0", "red1"],
    (2, 3): ["aexp0", "aexp1", "C0"],
    (3, 0): ["C1", "D0", "pre2", "red2"], (3, 1): ["aexp2", "pre3", "red3", "C2", "D1"],
    (3, 2): ["aexp3", "C3", "D2"], (3, 3): ["D3", "lst"],
    (4, 0): ["lrs", "qk3"], (4, 1): ["lap", "evA3"], (4, 2): ["evB3", "E0", "bo0"], (4, 3): ["E1", "bo1"],
    (5, 0): ["E2", "bo2"], (5, 1): ["E3", "bo3"],
    (6, 0): ["qk4"], (6, 1): ["evA4"], (6, 3): ["evB4"],
    (7, 2): ["V0"],
}
TAIL = ["V1", "pv", "evV0", "V2", "evV1", "V3", "evV2", "evV3",
        "O0", "O1", "O2", "O3", "yrs"]
PROLOGUE = ["A0", "A1", "B0", "A2", "B1", "A3", "B2", "B3", "nbm", "N", "pre0", "pre1", "red0", "red1",
            "aexp0", "aexp1", "C0", "C1", "D0", "pre2", "red2", "aexp2", "pre3", "red3", "C2", "D1", "aexp3",
            "C3", "D2", "D3", "lst", "lrs", "weights", "lap", "E0", "bo0", "E1", "bo1", "E2", "bo2", "E3", "bo3",
            "qk4", "evA4", "evB4", "V0", "V1", "evV0", "V2", "evV1", "V3", "evV2", "evV3"]


class Round:

    def __init__(self, pair, odd, uses, prologue=False, more=True, first=False):
        self.pair, self.odd, self.uses = pair, odd, uses
        self.prologue, self.more, self.first = prologue, more, first

    def n(self, per_graph, extra):
        return self.pair * (2 * per_graph) + (self.odd * per_graph + extra)

    def nx(self, per_graph, extra):
        return self.n(per_graph, per_graph + extra)

    def ring(self, name, extra=0):
        i = self.uses.index(name) + extra
        return i if self.prologue else self.n(len(ROUND), len(FIRST_LAYER) + i)

    def bank(self, name):
        return self.uses.index(name) % 2

    def pieces(self, names):
        for name in names:
            kind, index = (name[:-1], int(name[-1])) if name[-1].isdigit() else (name, 0)
            if kind in ("qk", "evA", "evB") and index == 4 and not self.more:
                continue
            if kind == "evV" and not self.more or kind in NEXT_ONLY and not self.more:
                continue
            if kind == "fin" and self.first:
                continue
            yield kind, index


def due(value):
    return not isinstance(value, int) or value > 0


def graph_layers(nc, x, adj, W, a, WqT, bq, WkT, bk, WvT, bv, WoT, bo, out):
    B, N, D = x.shape
    F1 = W.shape[1]
    T = N // P
    C = D // P
    DH = D // HEADS
    SCALE = float(DH) ** -0.5
    assert N == 512 and D == 512 and F1 == 256 and T == 4 and DH == 64 and B % 2 == 0 and B >= 6
    x_rows = x.rearrange("b n d -> (b n) d")
    out_rows = out.rearrange("b n d -> (b n) d")

    with ExitStack() as ctx:
        def sb(name, shape, dt=F32):
            return ctx.enter_context(nc.sbuf_tensor(name, shape, dt))

        def bank(name):
            return ctx.enter_context(nc.psum_tensor(name, [P, 512], F32))

        def sem(name):
            return ctx.enter_context(nc.semaphore(name))

        w0 = sb("w0", [P, 2, C, F1], F32R)
        wq = sb("wq", [P, 2, C, D], F32R)
        wk = sb("wk", [P, 2, C, D], F32R)
        wv = sb("wv", [P, 2, C, D], F32R)
        wo = sb("wo", [P, 2, C, D], F32R)
        mask0 = sb("mask0", [P, T, N])
        mask1 = sb("mask1", [P, T, N], BF16)
        ident = sb("ident", [P, P])
        a_wide = sb("a_wide", [P, 2, F1])
        bo_wide = sb("bo_wide", [P, D])
        bq_col = sb("bq_col", [P, 4])
        bk_col = sb("bk_col", [P, 4])
        bv_col = sb("bv_col", [P, 4])
        minus_half = sb("minus_half", [P, T])
        gate_dve = sb("gate_dve", [P, 2 * T])
        zero = sb("zero", [P, 1])
        tokens = [sb(f"tokens{i}", [P, T, D]) for i in range(2)]
        turned = sb("turned", [P, 2, 2, C, P], F32R)
        h0 = sb("h0", [P, 2, T, F1], F32R)
        n_wide = sb("n_wide", [P, N])
        alpha = sb("alpha", [P, 2, N])
        self_term = sb("self_term", [P, T])
        neigh_term = sb("neigh_term", [P, T])
        a_negmax = sb("a_negmax", [P, T])
        a_sum = sb("a_sum", [P, T])
        a_rsum = sb("a_rsum", [P, T])
        x1T = sb("x1T", [P, 2, C, N], F32R)
        q_st = sb("q_st", [P, 3, N], F32R)
        k_st = sb("k_st", [P, 3, 2, N], F32R)
        v_st = sb("v_st", [P, T, HEADS, 2 * DH], F32R)
        prob = sb("prob", [P, T, N])
        probT = sb("probT", [P, 2, 2, T, 2 * P], F32R)
        o_pair = sb("o_pair", [P, N])
        oT = sb("oT", [P, 2, C, N], F32R)
        negmax = sb("negmax", [P, T])
        psum_row = sb("psum_row", [P, T])
        rsum = sb("rsum", [P, T])
        stats = [sb(f"stats{i}", [P, T, 6]) for i in range(2)]
        meanvar = [sb(f"meanvar{i}", [P, T, 2]) for i in range(2)]
        var_eps = [sb(f"var_eps{i}", [P, T]) for i in range(2)]
        neg_mean = [sb(f"neg_mean{i}", [P, T]) for i in range(2)]
        rstd = [sb(f"rstd{i}", [P, T]) for i in range(2)]
        shift = [sb(f"shift{i}", [P, T]) for i in range(2)]

        S_bank = [bank(f"S_bank{i}") for i in range(2)]
        T_bank = [bank(f"T_bank{i}") for i in range(2)]
        O_bank = bank("O_bank")
        R_bank = [bank(f"R_bank{i}") for i in range(2)]
        L_bank = bank("L_bank")

        x_loaded = [sem(f"x_loaded{i}") for i in range(T)]
        y_stored = [sem(f"y_stored{i}") for i in range(T)]
        w_loaded = [sem(f"w_loaded{i}") for i in range(5)]
        adj_loaded, small_loaded = sem("adj_loaded"), sem("small_loaded")
        ident_built, masks_built = sem("ident_built"), sem("masks_built")
        w_hi, w_lo = sem("w_hi"), sem("w_lo")
        ring_mm, ring_done = sem("ring_mm"), sem("ring_done")
        turn_mm, turn_hi, turn_done = sem("turn_mm"), sem("turn_hi"), sem("turn_done")
        h_hi, h_lo, dots_done = sem("h_hi"), sem("h_lo"), sem("dots_done")
        nb_wide = sem("nb_wide")
        a_pre, a_leaky, a_red, a_exp, a_inv = (sem("a_pre"), sem("a_leaky"), sem("a_red"),
                                               sem("a_exp"), sem("a_inv"))
        x1_ready, bo_added = sem("x1_ready"), sem("bo_added")
        ln_dve = [sem(f"ln_dve{i}") for i in range(2)]
        ln_pool = [sem(f"ln_pool{i}") for i in range(2)]
        qk_hi, qk_lo = sem("qk_hi"), sem("qk_lo")
        k_twice = [sem("k_twice_a"), sem("k_twice_b")]
        v_hi = sem("v_hi")
        s_mm, s_red, p_exp, p_inv, p_norm = (sem("s_mm"), sem("s_red"), sem("p_exp"),
                                             sem("p_inv"), sem("p_norm"))
        t_mm, t_hi = sem("t_mm"), sem("t_hi")
        t_lo = [sem(f"t_lo{i}") for i in range(2)]
        pv_mm = [sem(f"pv_mm{i}") for i in range(2)]
        o_lows, o_sum, o_hi, o_lo = sem("o_lows"), sem("o_sum"), sem("o_hi"), sem("o_lo")
        y_ready = sem("y_ready")

        SMALL = 6 * 16
        IDENT = 3
        prologue = Round(-1, 1, FIRST_LAYER, prologue=True)
        final = Round(B // 2, 0, ROUND)

        def slot_of(h):
            return h % HEADS % 3

        def rows_of(h):
            return slice(DH * (h % 2), DH * (h % 2) + DH), slice(DH - DH * (h % 2), 2 * DH - DH * (h % 2))

        SLOT_FREE = {1: (0, 4), 2: (8, 12), 3: (16, 20), 4: (28, 32)}

        block = ctx.enter_context(nc.Block())

        @block.sync
        def _(sp):
            def load_tokens(dst, g_rows, i):
                sp.dma_start(dst[:, i, :], x_rows[g_rows, :]).then_inc(x_loaded[i], 16)

            for i in range(T):
                load_tokens(tokens[0], slice(i * P, i * P + P), i)
                if i == 0:
                    sp.dma_start(prob[:, 0:2, :].rearrange("p a b -> p (a b)").rearrange("p (c f) -> p c f", c=C),
                                 W.rearrange("(c p) f -> p c f", p=P)).then_inc(w_loaded[0], 16)
                    for j in range(2):
                        sp.dma_start(a_wide[:, j, :], a[j, :, 0].partition_broadcast(P)).then_inc(small_loaded, 16)
                    sp.dma_start(bo_wide[:, :], bo.partition_broadcast(P)).then_inc(small_loaded, 16)
                    for dst, src in ((bq_col, bq), (bk_col, bk), (bv_col, bv)):
                        sp.dma_start(dst[:, :], src).then_inc(small_loaded, 16)
            sp.dma_start(mask0[:, :, :].bitcast(I32), adj.rearrange("(t p) k -> p t k", p=P)).then_inc(adj_loaded, 16)
            for j, w in enumerate((WqT, WkT, WvT, WoT)):
                stage = tokens[1] if j % 2 == 0 else prob
                if j == 1:
                    sp.wait_ge(w_lo, 1)
                if j >= 2:
                    sp.wait_ge(w_lo, j)
                sp.dma_start(stage[:, :, :], w.rearrange("(c p) n -> p c n", p=P)).then_inc(w_loaded[1 + j], 16)

            def double_k(R, pair, which):
                h = 2 * pair + which
                own, other = rows_of(which)
                if which == 0:
                    sp.wait_ge(qk_lo, R.n(8, 2 * pair + 2))
                else:
                    sp.wait_ge(ring_done, R.ring(f"k{pair % 4}", 1))
                sp.dma_start(k_st[other, slot_of(h), :, :].bitcast(F32),
                             k_st[own, slot_of(h), :, :].bitcast(F32)).then_inc(k_twice[which], 16)

            def extra(R, names):
                for kind, i in R.pieces(names):
                    if kind == "evA":
                        double_k(R, i, 0)
                    if kind == "evB":
                        double_k(R, i, 1)

            def run_round(R):
                for h in range(HEADS):
                    for t in range(T):
                        if (h, t) == (0, 1) and R.more:
                            for i in range(T):
                                if R.first:
                                    sp.wait_ge(w_lo, 4)
                                else:
                                    sp.wait_ge(y_stored[i], R.n(16, 0))
                                load_tokens(tokens[1 - R.odd], bass.ds(R.n(N, N + i * P), P)
                                            if not isinstance(R.pair, int) else
                                            slice(R.n(N, N + i * P), R.n(N, N + i * P) + P), i)
                        extra(R, PLAN.get((h, t), []))

            extra(prologue, PROLOGUE)
            run_round(Round(0, 0, ROUND, first=True))
            run_round(Round(0, 1, ROUND))
            with sp.Fori(1, B // 2 - 1) as pair:
                run_round(Round(pair, 0, ROUND))
                run_round(Round(pair, 1, ROUND))
            run_round(Round(B // 2 - 1, 0, ROUND))
            run_round(Round(B // 2 - 1, 1, LAST_ROUND, more=False))
            for i in range(T):
                sp.wait_ge(y_stored[i], 16 * B)

        @block.tensor
        def _(pe):
            def ring(R, name):
                if due(R.ring(name, -1)):
                    pe.wait_ge(ring_done, R.ring(name, -1))
                return R_bank[R.bank(name)]

            def turn_free(R, name):
                if due(R.nx(13, TURNS.index(name))):
                    pe.wait_ge(turn_done, R.nx(13, TURNS.index(name)))

            def turn4(src):
                for c in range(4):
                    last = pe.transpose(L_bank[:, c * P:(c + 1) * P], src[:, c * P:(c + 1) * P], ident[:, :])
                last.then_inc(turn_mm, 1)

            def project(bank_ap, stationary, moving, done=ring_mm):
                todo = [(c, s, m) for c in range(C) for s, m in PARTS]
                for c, s, m in todo:
                    last = pe.matmul(bank_ap, stationary(s, c), moving(m, c), start=(c, s, m) == todo[0],
                                     stop=(c, s, m) == todo[-1])
                last.then_inc(done, 1)

            def piece(R, kind, i):
                if kind == "A":
                    pe.wait_ge(x_loaded[i], R.nx(16, 16))
                    turn_free(R, f"A{i}")
                    turn4(tokens[1 - R.odd][:, i, :])
                if kind == "B":
                    out_b = ring(R, f"B{i}")
                    pe.wait_ge(turn_done, R.nx(13, i + 1))
                    project(out_b[:, 0:F1], lambda s, c: turned[:, i % 2, s, c, :], lambda m, c: w0[:, m, c, :])
                if kind == "N":
                    pe.wait_ge(nb_wide, R.nx(4, 4))
                    turn_free(R, "N")
                    turn4(n_wide[:, :])
                if kind == "C":
                    pe.wait_ge(a_exp, R.nx(4, i + 1))
                    turn_free(R, f"C{i}")
                    turn4(alpha[:, i % 2, :])
                if kind == "D":
                    out_b = ring(R, f"D{i}")
                    pe.wait_ge(turn_done, R.nx(13, 6 + i))
                    project(out_b[:, 0:F1], lambda s, c: turned[:, i % 2, s, c, :], lambda m, c: h0[:, m, c, :])
                if kind == "E":
                    pe.wait_ge(x1_ready, R.nx(4, i + 1))
                    turn_free(R, f"E{i}")
                    turn4(tokens[1 - R.odd][:, i, :])
                if kind == "weights":
                    pe.wait_ge(w_lo, 5)
                if kind == "qk":
                    if i == 4:
                        pe.wait_ge(turn_done, R.nx(13, 13))
                    c0 = (i % 4) * P
                    for name, w in ((f"q{i % 4}", wq), (f"k{i % 4}", wk)):
                        out_b = ring(R, name)
                        project(out_b[:, :], lambda s, c: w[:, s, c, c0:c0 + P], lambda m, c: x1T[:, m, c, :])
                if kind == "V":
                    out_b = ring(R, f"V{i}")
                    project(out_b[:, :], lambda s, c: x1T[:, s, c, i * P:(i + 1) * P], lambda m, c: wv[:, m, c, :])
                if kind == "O":
                    if i == 0:
                        pe.wait_ge(o_lo, R.n(4, 4))
                    out_b = ring(R, f"O{i}")
                    project(out_b[:, :], lambda s, c: oT[:, s, c, i * P:(i + 1) * P], lambda m, c: wo[:, m, c, :])
                if kind == "pv":
                    weigh(R, HEADS - 1, 1)

            def scores(R, h, t):
                if t == 0:
                    pe.wait_ge(k_twice[h % 2], R.n(64, 16 * (h // 2 + 1)))
                if due(R.n(32, 4 * h + t - 1)):
                    pe.wait_ge(s_red, R.n(32, 4 * h + t - 1))
                for part in (HI, LO):
                    last = pe.matmul(S_bank[t % 2][:, :], q_st[:, slot_of(h), t * P:(t + 1) * P],
                                     k_st[:, slot_of(h), part, :], start=part == HI, stop=part == LO)
                last.then_inc(s_mm, 1)

            def turn_probs(R, h, t):
                pe.wait_ge(p_norm, R.n(32, 4 * h + t + 1))
                if due(R.n(16, 2 * h + t // 2)):
                    pe.wait_ge(t_lo[t % 2], R.n(16, 2 * h + t // 2))
                for c in range(T):
                    last = pe.transpose(T_bank[t % 2][:, c * P:(c + 1) * P], prob[:, t, c * P:(c + 1) * P],
                                        ident[:, :])
                last.then_inc(t_mm, 1)

            def weigh(R, h, half):
                for b in range(2):
                    pe.wait_ge(t_lo[b], R.n(16, 2 * h + half + 1))
                if half == 0 and h == 0:
                    pe.wait_ge(ring_done, R.n(len(ROUND), len(FIRST_LAYER)))
                if half == 0 and due(R.n(8, h)):
                    pe.wait_ge(o_sum, R.n(8, h))
                todo = [(c, s) for c in range(T) for s in (HI, LO)]
                for c, s in todo:
                    last = pe.matmul(O_bank[:, half * 2 * P:(half + 1) * 2 * P], v_st[:, c, h, :],
                                     probT[:, half, s, c, :], start=(c, s) == todo[0], stop=(c, s) == todo[-1])
                last.then_inc(pv_mm[half], 1)

            def run_round(R):
                for h in range(HEADS):
                    for t in range(T):
                        turn_probs(R, h, t)
                        if h < HEADS - 1 or R.more:
                            scores(R, h + 1, t)
                        if t == 1 and h > 0:
                            weigh(R, h - 1, 1)
                        if t == 3:
                            weigh(R, h, 0)
                        for kind, i in R.pieces(PLAN.get((h, t), [])):
                            piece(R, kind, i)
                for kind, i in R.pieces(TAIL):
                    piece(R, kind, i)

            pe.wait_ge(ident_built, IDENT)
            for kind, i in prologue.pieces(PROLOGUE):
                if (kind, i) == ("B", 0):
                    pe.wait_ge(w_lo, 1)
                piece(prologue, kind, i)
            for t in range(T):
                scores(prologue, HEADS, t)
            run_round(Round(0, 0, ROUND, first=True))
            run_round(Round(0, 1, ROUND))
            with pe.Fori(1, B // 2 - 1) as pair:
                run_round(Round(pair, 0, ROUND))
                run_round(Round(pair, 1, ROUND))
            run_round(Round(B // 2 - 1, 0, ROUND))
            run_round(Round(B // 2 - 1, 1, LAST_ROUND, more=False))

        @block.scalar
        def _(act):
            def split_hi(dst, src, done):
                act.activation(dst, src, ACT.Copy).then_inc(done, 1)

            def head_hi(R, pair, which):
                h = 2 * pair + which
                own, _ = rows_of(which)
                free = SLOT_FREE[pair][which]
                if due(R.n(32, free)):
                    act.wait_ge(s_mm, R.n(32, free))
                p4 = pair % 4
                for j, (name, b_col) in enumerate(((f"q{p4}", bq_col), (f"k{p4}", bk_col))):
                    act.wait_ge(ring_mm, R.ring(name, 1))
                    dst = (q_st[own, slot_of(h), :], k_st[own, slot_of(h), HI, :])[j]
                    act.activation(dst, R_bank[R.bank(name)][own, :], ACT.Identity,
                                   bias=b_col[own, p4:p4 + 1]).then_inc(qk_hi, 1)

            def store(R, i):
                act.wait_ge(y_ready, R.n(4, i - 3))
                rows = (slice(R.n(N, i * P - N), R.n(N, i * P - N) + P) if isinstance(R.pair, int)
                        else bass.ds(R.n(N, i * P - N), P))
                act.dma_start(out_rows[rows, :], tokens[1 - R.odd][:, i, :]).then_inc(y_stored[i], 16)

            def piece(R, kind, i):
                if kind in ("A", "C"):
                    j = TURNS.index(f"{kind}{i}")
                    act.wait_ge(turn_mm, R.nx(13, j + 1))
                    reader = {"A2": "B0", "A3": "B1", "C0": "B2", "C1": "B3", "C2": "D0", "C3": "D1"}.get(f"{kind}{i}")
                    if reader:
                        act.wait_ge(ring_mm, R.ring(reader, 1))
                    split_hi(turned[:, i % 2, HI, :, :], L_bank[:, :].rearrange("p (c t) -> p c t", c=C), turn_hi)
                if kind == "B":
                    act.wait_ge(ring_mm, R.ring(f"B{i}", 1))
                    split_hi(h0[:, HI, i, :], R_bank[R.bank(f"B{i}")][:, 0:F1], h_hi)
                if kind == "pre":
                    if i == 0:
                        act.wait_ge(turn_done, R.nx(13, 5))
                    if i >= 2:
                        act.wait_ge(turn_mm, R.nx(13, 6 + i - 2))
                    act.activation(alpha[:, i % 2, :], n_wide[:, :], ACT.Identity,
                                   bias=self_term[:, i:i + 1]).then_inc(a_pre, 1)
                if kind == "aexp":
                    act.wait_ge(a_red, R.nx(4, i + 1))
                    act.activation(alpha[:, i % 2, :], alpha[:, i % 2, :], ACT.Exp, bias=a_negmax[:, i:i + 1],
                                   scale=-1.0, accum_out=a_sum[:, i:i + 1]).then_inc(a_exp, 1)
                if kind == "lap":
                    act.wait_ge(ln_pool[0], R.nx(2, 2))
                    for j in range(T):
                        t_ap = tokens[1 - R.odd][:, j, :]
                        act.activation(t_ap, t_ap, ACT.Identity, bias=shift[0][:, j:j + 1],
                                       scale=rstd[0][:, j:j + 1]).then_inc(x1_ready, 1)
                if kind == "E":
                    act.wait_ge(turn_mm, R.nx(13, 10 + i))
                    if i == 0 and not R.prologue:
                        act.wait_ge(ring_mm, R.ring("k3", 1))
                    split_hi(x1T[:, HI, :, i * P:(i + 1) * P], L_bank[:, :].rearrange("p (c t) -> p c t", c=C), turn_hi)
                if kind == "weights":
                    for j, w in enumerate((wq, wk, wv, wo)):
                        act.wait_ge(w_loaded[1 + j], 16)
                        stage = tokens[1] if j % 2 == 0 else prob
                        split_hi(w[:, HI, :, :], stage[:, :, :], w_hi)
                if kind == "evA":
                    head_hi(R, i, 0)
                if kind == "evB":
                    head_hi(R, i, 1)
                if kind == "evV":
                    act.wait_ge(ring_mm, R.ring(f"V{i}", 1))
                    if i == 0 and not R.prologue:
                        act.wait_ge(pv_mm[1], R.n(8, 8))
                    split_hi(v_st[:, i, :, 0:DH], R_bank[R.bank(f"V{i}")][:, :].rearrange("p (h d) -> p h d", d=DH), v_hi)
                if kind == "pv":
                    head_lows(R, HEADS - 1)
                    pair_hi(R, HEADS // 2 - 1)
                if kind == "fin":
                    act.wait_ge(ln_pool[1], R.n(2, 0))
                    for j in range(T):
                        t_ap = tokens[1 - R.odd][:, j, :]
                        act.activation(t_ap, t_ap, ACT.Identity, bias=shift[1][:, j:j + 1],
                                       scale=rstd[1][:, j:j + 1]).then_inc(y_ready, 1)
                    for j in range(T):
                        store(R, j)

            def exps(R, h, t):
                act.wait_ge(s_red, R.n(32, 4 * h + t + 1))
                act.activation(prob[:, t, :], prob[:, t, :], ACT.Exp, bias=negmax[:, t:t + 1], scale=-1.0,
                               accum_out=psum_row[:, t:t + 1]).then_inc(p_exp, 1)

            def probs_hi(R, h, t):
                if due(R.n(8, h)):
                    act.wait_ge(pv_mm[t // 2], R.n(8, h))
                act.wait_ge(t_mm, R.n(32, 4 * h + t + 1))
                split_hi(probT[:, t // 2, HI, :, (t % 2) * P:(t % 2 + 1) * P],
                         T_bank[t % 2][:, :].rearrange("p (c q) -> p c q", c=T), t_hi)

            def head_lows(R, h):
                own, _ = rows_of(h)
                if due(R.n(4, h // 2)):
                    act.wait_ge(o_lo, R.n(4, h // 2))
                act.wait_ge(pv_mm[1], R.n(8, h + 1))
                act.activation(o_pair[own, :], O_bank[DH:2 * DH, :], ACT.Identity,
                               bias=bv_col[own, h // 2:h // 2 + 1]).then_inc(o_lows, 1)

            def pair_hi(R, pair):
                if due(R.n(4, 0)):
                    act.wait_ge(ring_mm, R.n(len(ROUND), len(FIRST_LAYER)))
                act.wait_ge(o_sum, R.n(8, 2 * pair + 2))
                split_hi(oT[:, HI, pair, :], o_pair[:, :], o_hi)

            def run_round(R):
                for h in range(HEADS):
                    for t in range(T):
                        probs_hi(R, h, t)
                        if h < HEADS - 1 or R.more:
                            exps(R, h + 1, t)
                        if t == 1 and h > 0:
                            head_lows(R, h - 1)
                        if t == 2 and h > 0 and h % 2 == 0:
                            pair_hi(R, h // 2 - 1)
                        for kind, i in R.pieces(PLAN.get((h, t), [])):
                            piece(R, kind, i)
                for kind, i in R.pieces(TAIL):
                    piece(R, kind, i)

            act.wait_ge(w_loaded[0], 16)
            split_hi(w0[:, HI, :, :].rearrange("p c f -> p (c f)"), prob[:, 0:2, :].rearrange("p a b -> p (a b)"), w_hi)
            act.wait_ge(small_loaded, SMALL)
            for kind, i in prologue.pieces(PROLOGUE):
                piece(prologue, kind, i)
            for t in range(T):
                exps(prologue, HEADS, t)
            run_round(Round(0, 0, ROUND, first=True))
            run_round(Round(0, 1, ROUND))
            with act.Fori(1, B // 2 - 1) as pair:
                run_round(Round(pair, 0, ROUND))
                run_round(Round(pair, 1, ROUND))
            run_round(Round(B // 2 - 1, 0, ROUND))
            run_round(Round(B // 2 - 1, 1, LAST_ROUND, more=False))
            piece(final, "fin", 0)

        @block.vector
        def _(dve):
            def gate(i):
                dve.memset(gate_dve[:, i:i + 1], 0.0)

            def split_lo(dst, src, hi, done):
                dve.tensor_tensor(dst, src, hi.bitcast(F32), ALU.subtract).then_inc(done, 1)

            def layer_stats(which, count, i, t_ap):
                dve.bn_stats(stats[which][:, i, :], t_ap).then_inc(ln_dve[which], 1)
                dve.wait_ge(ln_dve[which], count(2 * i + 1))
                gate(i)
                dve.bn_aggr(meanvar[which][:, i, :], stats[which][:, i, :]).then_inc(ln_dve[which], 1)

            def layer_scales(which, count):
                dve.wait_ge(ln_dve[which], count(2 * T))
                dve.tensor_scalar(var_eps[which][:, :], meanvar[which][:, :, 1], EPS, None,
                                  ALU.add).then_inc(ln_dve[which], 1)
                dve.tensor_scalar(neg_mean[which][:, :], meanvar[which][:, :, 0], -1.0, None,
                                  ALU.mult).then_inc(ln_dve[which], 1)

            def head_lo(R, pair, which):
                h = 2 * pair + which
                own, other = rows_of(which)
                p4 = pair % 4
                for j, (name, b_col) in enumerate(((f"q{p4}", bq_col), (f"k{p4}", bk_col))):
                    dve.wait_ge(qk_hi, R.n(16, 4 * (pair - 1) + 2 * which + j + 1 + 4))
                    src = R_bank[R.bank(name)][own, :]
                    hi = (q_st[own, slot_of(h), :], k_st[own, slot_of(h), HI, :])[j]
                    dst = (q_st[other, slot_of(h), :], k_st[own, slot_of(h), LO, :])[j]
                    ins = dve.scalar_tensor_tensor(out=dst, in0=src, scalar=b_col[own, p4:p4 + 1],
                                                   in1=hi.bitcast(F32), op0=ALU.add, op1=ALU.subtract)
                    ins.then_inc(qk_lo if which == 0 else ring_done, 1)

            def piece(R, kind, i):
                if kind in ("A", "C"):
                    j = TURNS.index(f"{kind}{i}")
                    if kind == "C":
                        dve.wait_ge(a_exp, R.nx(4, i + 1))
                        dve.reciprocal(a_rsum[:, i:i + 1], a_sum[:, i:i + 1]).then_inc(a_inv, 1)
                    dve.wait_ge(turn_hi, R.nx(12, j + 1 - (kind == "C")))
                    split_lo(turned[:, i % 2, LO, :, :], L_bank[:, :].rearrange("p (c t) -> p c t", c=C),
                             turned[:, i % 2, HI, :, :], turn_done)
                if kind == "B":
                    src = R_bank[R.bank(f"B{i}")][:, 0:F1]
                    dve.wait_ge(h_hi, R.nx(4, i + 1))
                    split_lo(h0[:, LO, i, :], src, h0[:, HI, i, :], h_lo)
                    if i > 0:
                        dve.wait_ge(dots_done, R.nx(8, 2 * i))
                    for j, dst in enumerate((self_term, neigh_term)):
                        dve.tensor_tensor_reduce(n_wide[:, j * F1:(j + 1) * F1], src, a_wide[:, j, :], 1.0, 0.0,
                                                 ALU.mult, ALU.add, dst[:, i:i + 1]).then_inc(dots_done, 1)
                    dve.tensor_tensor(tokens[1 - R.odd][:, i, F1:D], src, tokens[1 - R.odd][:, i, F1:D],
                                      ALU.add).then_inc(ring_done, 1)
                if kind == "N":
                    dve.wait_ge(turn_mm, R.nx(13, 5))
                    dve.tensor_copy(n_wide[:, :], L_bank[:, :]).then_inc(turn_done, 1)
                if kind == "red":
                    al = alpha[:, i % 2, :]
                    dve.wait_ge(a_pre, R.nx(4, i + 1))
                    dve.scalar_tensor_tensor(out=al, in0=al, scalar=LEAK, in1=al, op0=ALU.mult,
                                             op1=ALU.max).then_inc(a_leaky, 1)
                    dve.wait_ge(a_leaky, R.nx(4, i + 1))
                    gate(T + i)
                    dve.tensor_tensor_reduce(al, al, mask0[:, i, :], -1.0, HUGE, ALU.add, ALU.min,
                                             a_negmax[:, i:i + 1]).then_inc(a_red, 1)
                if kind == "D":
                    t_ap = tokens[1 - R.odd][:, i, 0:F1]
                    dve.wait_ge(a_inv, R.nx(4, i + 1))
                    dve.wait_ge(ring_mm, R.ring(f"D{i}", 1))
                    dve.scalar_tensor_tensor(out=t_ap, in0=R_bank[R.bank(f"D{i}")][:, 0:F1], scalar=a_rsum[:, i:i + 1],
                                             in1=t_ap, op0=ALU.mult, op1=ALU.add).then_inc(ring_done, 1)
                if kind == "lst":
                    for j in range(T):
                        dve.wait_ge(ring_done, R.ring(f"D{j}", 1))
                        layer_stats(0, lambda c: R.nx(10, c), j, tokens[1 - R.odd][:, j, :])
                if kind == "lrs":
                    layer_scales(0, lambda c: R.nx(10, c))
                if kind == "E":
                    dve.wait_ge(turn_hi, R.nx(12, 9 + i))
                    split_lo(x1T[:, LO, :, i * P:(i + 1) * P], L_bank[:, :].rearrange("p (c t) -> p c t", c=C),
                             x1T[:, HI, :, i * P:(i + 1) * P], turn_done)
                if kind == "weights":
                    for j, w in enumerate((wq, wk, wv, wo)):
                        dve.wait_ge(w_hi, 2 + j)
                        stage = tokens[1] if j % 2 == 0 else prob
                        split_lo(w[:, LO, :, :], stage[:, :, :], w[:, HI, :, :], w_lo)
                if kind == "evA":
                    head_lo(R, i, 0)
                if kind == "evB":
                    head_lo(R, i, 1)
                if kind == "evV":
                    dve.wait_ge(v_hi, R.nx(4, i + 1))
                    split_lo(v_st[:, i, :, DH:2 * DH], R_bank[R.bank(f"V{i}")][:, :].rearrange("p (h d) -> p h d", d=DH),
                             v_st[:, i, :, 0:DH], ring_done)
                if kind == "pv":
                    head_sum(R, HEADS - 1)
                if kind == "O":
                    t_ap = tokens[R.odd][:, i, :]
                    dve.wait_ge(bo_added, R.n(4, i + 1))
                    dve.wait_ge(ring_mm, R.ring(f"O{i}", 1))
                    dve.tensor_tensor(t_ap, R_bank[R.bank(f"O{i}")][:, :], t_ap, ALU.add).then_inc(ring_done, 1)
                    dve.wait_ge(ring_done, R.ring(f"O{i}", 1))
                    layer_stats(1, lambda c: R.n(10, c), i, t_ap)
                if kind == "yrs":
                    layer_scales(1, lambda c: R.n(10, c))

            def reduce_scores(R, h, t, unit_before=None):
                if due(R.n(32, 4 * (h - 1) + t + 1)) and not R.prologue:
                    dve.wait_ge(t_mm, R.n(32, 4 * (h - 1) + t + 1))
                dve.wait_ge(s_mm, R.n(32, 4 * h + t + 1))
                if unit_before is not None:
                    invert_sums(R, *unit_before)
                dve.tensor_tensor_reduce(prob[:, t, :], S_bank[t % 2][:, :], mask1[:, t, :], -SCALE, HUGE, ALU.add,
                                         ALU.min, negmax[:, t:t + 1]).then_inc(s_red, 1)

            def invert_sums(R, h, t):
                dve.wait_ge(p_exp, R.n(32, 4 * h + t + 1))
                dve.reciprocal(rsum[:, t:t + 1], psum_row[:, t:t + 1]).then_inc(p_inv, 1)

            def probs_lo(R, h, t):
                dve.wait_ge(t_hi, R.n(32, 4 * h + t + 1))
                cols = slice((t % 2) * P, (t % 2 + 1) * P)
                split_lo(probT[:, t // 2, LO, :, cols], T_bank[t % 2][:, :].rearrange("p (c q) -> p c q", c=T),
                         probT[:, t // 2, HI, :, cols], t_lo[t % 2])

            def head_sum(R, h):
                own, _ = rows_of(h)
                dve.wait_ge(o_lows, R.n(8, h + 1))
                dve.tensor_tensor(o_pair[own, :], O_bank[0:DH, :], o_pair[own, :], ALU.add).then_inc(o_sum, 1)

            def run_round(R):
                for h in range(HEADS):
                    for t in range(T):
                        probs_lo(R, h, t)
                        before = (h + 1, t - 1) if t > 0 else (h, T - 1) if not (h == 0 and R.first) else None
                        if h < HEADS - 1 or R.more:
                            reduce_scores(R, h + 1, t, before)
                        elif t == 0:
                            invert_sums(R, *before)
                        if t == 1 and h > 0:
                            head_sum(R, h - 1)
                        for kind, i in R.pieces(PLAN.get((h, t), [])):
                            piece(R, kind, i)
                for kind, i in R.pieces(TAIL):
                    piece(R, kind, i)

            dve.memset(minus_half[:, :], -0.5).then_inc(masks_built, 1)
            dve.wait_ge(adj_loaded, 16)
            dve.tensor_scalar(mask1[:, :, :], mask0[:, :, :].bitcast(I32), 0.0, MASKED, ALU.is_equal,
                              ALU.mult).then_inc(masks_built, 1)
            dve.tensor_scalar(mask0[:, :, :], mask0[:, :, :].bitcast(I32), -NEG, NEG, ALU.mult,
                              ALU.add).then_inc(masks_built, 1)
            dve.wait_ge(w_hi, 1)
            split_lo(w0[:, LO, :, :].rearrange("p c f -> p (c f)"), prob[:, 0:2, :].rearrange("p a b -> p (a b)"),
                     w0[:, HI, :, :].rearrange("p c f -> p (c f)"), w_lo)
            dve.wait_ge(small_loaded, SMALL)
            for kind, i in prologue.pieces(PROLOGUE):
                piece(prologue, kind, i)
            for t in range(T):
                reduce_scores(prologue, HEADS, t)
                invert_sums(prologue, HEADS, t)
            run_round(Round(0, 0, ROUND, first=True))
            run_round(Round(0, 1, ROUND))
            with dve.Fori(1, B // 2 - 1) as pair:
                run_round(Round(pair, 0, ROUND))
                run_round(Round(pair, 1, ROUND))
            run_round(Round(B // 2 - 1, 0, ROUND))
            run_round(Round(B // 2 - 1, 1, LAST_ROUND, more=False))

        @block.gpsimd
        def _(pool):
            def normalise(R, h, t):
                pool.wait_ge(p_inv, R.n(32, 4 * h + t + 1))
                pool.tensor_tensor(prob[:, t, :], prob[:, t, :], rsum[:, t:t + 1].to_broadcast([P, N]),
                                   ALU.mult).then_inc(p_norm, 1)

            def scales(which, full, half):
                pool.wait_ge(ln_dve[which], full)
                pool.tensor_tensor(rstd[which][:, :], var_eps[which][:, :], minus_half[:, :],
                                   ALU.pow).then_inc(ln_pool[which], 1)
                pool.wait_ge(ln_pool[which], half)
                pool.tensor_tensor(shift[which][:, :], neg_mean[which][:, :], rstd[which][:, :],
                                   ALU.mult).then_inc(ln_pool[which], 1)

            def pair_lo(R, pair):
                pool.wait_ge(o_hi, R.n(4, pair + 1))
                pool.tensor_tensor(oT[:, LO, pair, :], o_pair[:, :], oT[:, HI, pair, :].bitcast(F32),
                                   ALU.subtract).then_inc(o_lo, 1)

            def piece(R, kind, i):
                if kind == "nbm":
                    pool.wait_ge(dots_done, R.nx(8, 8))
                    for j in range(T):
                        pool.tensor_tensor(n_wide[:, j * P:(j + 1) * P], neigh_term[:, j:j + 1].to_broadcast([P, P]),
                                           zero[:, :].to_broadcast([P, P]), ALU.add).then_inc(nb_wide, 1)
                if kind == "lrs":
                    scales(0, R.nx(10, 10), R.nx(2, 1))
                if kind == "yrs":
                    scales(1, R.n(10, 10), R.n(2, 1))
                if kind == "bo":
                    pool.wait_ge(turn_mm, R.nx(13, 10 + i))
                    t_ap = tokens[1 - R.odd][:, i, :]
                    pool.tensor_tensor(t_ap, t_ap, bo_wide[:, :], ALU.add).then_inc(bo_added, 1)
                if kind == "pv":
                    pair_lo(R, HEADS // 2 - 1)

            def run_round(R):
                for h in range(HEADS):
                    for t in range(T):
                        if t > 0 and (h < HEADS - 1 or R.more):
                            normalise(R, h + 1, t - 1)
                        if t == 0 and not (h == 0 and R.first):
                            normalise(R, h, T - 1)
                        if t == 2 and h > 0 and h % 2 == 0:
                            pair_lo(R, h // 2 - 1)
                        for kind, i in R.pieces(PLAN.get((h, t), [])):
                            piece(R, kind, i)
                for kind, i in R.pieces(TAIL):
                    piece(R, kind, i)

            pool.memset(zero[:, :], 0.0).then_inc(ident_built, 1)
            pool.memset(ident[:, :], 0.0).then_inc(ident_built, 1)
            pool.wait_ge(ident_built, 2)
            pool.affine_select(out=ident[:, :], in_=ident[:, :], compare_op=ALU.not_equal, fill=1.0, base=0,
                               pattern=[[-1, P]], channel_multiplier=1).then_inc(ident_built, 1)
            pool.wait_ge(small_loaded, SMALL)
            pool.wait_ge(masks_built, 1)
            for kind, i in prologue.pieces(PROLOGUE):
                piece(prologue, kind, i)
            for t in range(T):
                normalise(prologue, HEADS, t)
            run_round(Round(0, 0, ROUND, first=True))
            run_round(Round(0, 1, ROUND))
            with pool.Fori(1, B // 2 - 1) as pair:
                run_round(Round(pair, 0, ROUND))
                run_round(Round(pair, 1, ROUND))
            run_round(Round(B // 2 - 1, 0, ROUND))
            run_round(Round(B // 2 - 1, 1, LAST_ROUND, more=False))


def kernel(x, adj, L0_gnn_W, L0_gnn_a, L1_gnn_Wq, L1_gnn_bq, L1_gnn_Wk, L1_gnn_bk, L1_gnn_Wv, L1_gnn_bv,
           L1_gnn_Wo, L1_gnn_bo):
    import numpy as np
    import concourse.bacc as bacc
    from concourse.bass_utils import run_bass_kernel_spmd

    def columns(b):
        return np.ascontiguousarray(np.asarray(b).reshape(-1, P).T)

    def turned(w):
        return np.ascontiguousarray(np.asarray(w).T)

    arrays = {
        "x": np.ascontiguousarray(x), "adj": np.ascontiguousarray(adj), "W": np.ascontiguousarray(L0_gnn_W),
        "a": np.ascontiguousarray(L0_gnn_a), "WqT": turned(L1_gnn_Wq), "bq": columns(L1_gnn_bq),
        "WkT": turned(L1_gnn_Wk), "bk": columns(L1_gnn_bk), "WvT": turned(L1_gnn_Wv), "bv": columns(L1_gnn_bv),
        "WoT": turned(L1_gnn_Wo), "bo": np.ascontiguousarray(L1_gnn_bo),
    }
    nc = bacc.Bacc("TRN2", target_bir_lowering=False, num_devices=1, dynamic_dma_scratch_size=1024)
    args = [nc.dram_tensor(name, v.shape, mybir.dt.from_np(v.dtype), kind="ExternalInput").ap()
            for name, v in arrays.items()]
    out = nc.dram_tensor("out", arrays["x"].shape, F32, kind="ExternalOutput").ap()
    graph_layers(nc, *args, out)
    r = run_bass_kernel_spmd(nc, [arrays], core_ids=[0])
    return r.results[0]["out"]
```

```python
from contextlib import ExitStack

import concourse.bass as bass
from concourse import mybir

ALU = mybir.AluOpType
ACT = mybir.ActivationFunctionType
F32 = mybir.dt.float32
F32R = mybir.dt.float32r
BF16 = mybir.dt.bfloat16
I32 = mybir.dt.int32

P = 128
HEADS = 8
EPS = 1e-5
LEAK = 0.2
MASKED = -3.0e38
HUGE = 3.0e38
HI, LO = 0, 1
PARTS = ((HI, HI), (HI, LO), (LO, HI))

FIRST_LAYER = ["D0", "D1", "D2", "D3", "V0", "V1", "V2", "V3", "q4", "k4", "q1"]
ROUND = ["k1", "O0", "O1", "O2", "O3", "q2", "k2", "D0", "D1", "W0", "W1", "W2", "W3", "D2", "D3",
         "q3", "k3", "V0", "V1", "V2", "V3", "q4", "k4", "q1"]
FIRST_ROUND = [u for u in ROUND if u[0] != "O"]
LAST_ROUND = ["k1", "O0", "O1", "O2", "O3", "q2", "k2", "W0", "W1", "W2", "W3", "q3", "k3"]
END = ["O0", "O1", "O2", "O3"]
RING0 = len(FIRST_LAYER) + len(FIRST_ROUND) - len(ROUND)
SOLO = ["A0", "B0", "A1", "B1", "A2", "B2", "A3", "B3", "N", "C0", "C1", "C2", "C3", "E0", "E1", "E2", "E3"]
SECOND_ONLY = set("AB") | {"nbm", "ld"}
NEXT_ONLY = set("NCDEV") | {"pre", "red", "aexp", "evD", "lst", "lrs", "lap", "bo", "evV"}
LAST_ONLY = {"pv", "O", "evO", "yst", "yrs", "fin"}

PLAN = {
    (0, 0): ["k1"],
    (0, 1): ["N", "pv", "evA1"],
    (0, 2): ["evB1", "pre0", "pre1"],
    (0, 3): ["O0", "red0", "evO0"],
    (1, 0): ["aexp0", "O1", "red1", "evO1"],
    (1, 1): ["C0", "aexp1", "O2", "evO2"],
    (1, 2): ["C1", "O3", "evO3", "pre2", "yst0"],
    (1, 3): ["q2", "pre3", "red2", "yst1"],
    (2, 0): ["aexp2", "k2", "red3", "yst2"],
    (2, 1): ["aexp3", "evA2"],
    (2, 2): ["evB2", "yst3", "yrs"],
    (2, 3): ["D0", "D1", "fin0", "evD0", "evD1"],
    (3, 0): ["C2", "W0", "W1", "fin1", "evW0", "evW1", "lst0"],
    (3, 1): ["C3", "W2", "W3", "fin2", "evW2", "evW3"],
    (3, 2): ["D2", "D3", "fin3", "evD2", "evD3", "lst1"],
    (3, 3): ["q3", "lst2", "lst3", "lrs", "ld0"],
    (4, 0): ["k3", "ld1"],
    (4, 1): ["evA3", "lap0"],
    (4, 2): ["E0", "lap1", "evB3", "ld2"],
    (4, 3): ["E1", "lap2", "lap3", "ld3"],
    (5, 0): ["V0", "E2", "evV0", "bo0"],
    (5, 1): ["V1", "E3", "evV1", "bo1"],
    (5, 2): ["V2", "V3", "A0", "evV2", "evV3", "bo2"],
    (5, 3): ["q4", "B0", "bo3"],
    (6, 0): ["k4", "A1"],
    (6, 1): ["B1", "evA4"],
    (6, 2): ["A2", "evB4"],
    (6, 3): ["B2"],
    (7, 0): ["A3"],
    (7, 1): ["B3"],
    (7, 2): ["nbm"],
    (7, 3): ["q1"],
}
START = ["A0", "B0", "A1", "B1", "A2", "B2", "A3", "B3", "nbm"]
PROLOGUE = ["N", "pre0", "pre1", "red0", "red1", "aexp0", "aexp1", "C0", "C1", "D0", "pre2", "red2", "aexp2",
            "pre3", "red3", "D1", "evD0", "C2", "evD1", "aexp3", "C3", "lst0", "lst1", "D2", "D3", "evD2", "evD3",
            "lst2", "lst3", "lrs", "weights", "lap0", "E0", "lap1", "E1", "lap2", "E2", "lap3", "E3",
            "bo0", "bo1", "bo2", "bo3", "V0", "V1", "evV0", "V2", "evV1", "V3", "evV2", "q4", "evV3", "k4",
            "evA4", "evB4", "A0", "B0", "A1", "B1", "A2", "B2", "A3", "B3", "nbm", "q1"]
ENDING = ["pv", "O0", "O1", "evO0", "O2", "yst0", "evO1", "O3", "yst1", "evO2", "evO3", "yst2", "yst3", "yrs",
          "fin0", "fin1", "fin2", "fin3"]


class Round:

    def __init__(self, i, k, uses=ROUND, last=True, more=True, load=True):
        self.i, self.k, self.uses = i, k, uses
        self.last, self.more, self.load = last, more, load
        self.prologue = uses is FIRST_LAYER
        self.ring0 = {id(FIRST_LAYER): len(ROUND), id(FIRST_ROUND): len(FIRST_LAYER),
                      id(END): RING0 + len(LAST_ROUND) - len(ROUND)}.get(id(uses), RING0)

    def n(self, per_graph, extra):
        return self.i * (3 * per_graph) + (self.k * per_graph + extra)

    def nx(self, per_graph, extra):
        return self.n(per_graph, per_graph + extra)

    def n2(self, per_graph, extra):
        return self.n(per_graph, 2 * per_graph + extra)

    def ring(self, name, extra=0):
        return self.n(len(ROUND), self.ring0 + self.uses.index(name) + extra)

    def bank(self, name):
        return (self.ring0 + self.uses.index(name)) % 2

    def buffer(self, ahead):
        return (self.k + ahead) % 3

    def slot(self, h):
        return (HEADS * self.k + h) % 3

    def rows(self, ahead, tile):
        first = self.n(512, 512 * ahead + P * tile)
        return slice(first, first + P) if isinstance(first, int) else bass.ds(first, P)

    def pieces(self, names):
        for name in names:
            kind, index = (name[:-1], int(name[-1])) if name[-1].isdigit() else (name, 0)
            ahead = kind in NEXT_ONLY or kind in ("q", "k", "evA", "evB") and index == 4 or name == "q1"
            if ((self.more or not ahead) and (self.last or kind not in LAST_ONLY)
                    and (self.load or kind not in SECOND_ONLY)):
                yield kind, index


def due(value):
    return not isinstance(value, int) or value > 0


def graph_layers(nc, x, adj, W, a, WqT, bq, WkT, bk, WvT, bv, WoT, bo, out):
    B, N, D = x.shape
    F1 = W.shape[1]
    T = N // P
    C = D // P
    DH = D // HEADS
    SCALE = float(DH) ** -0.5
    assert N == 512 and D == 512 and F1 == 256 and T == 4 and DH == 64 and B % 3 == 2 and B >= 8
    x_rows = x.rearrange("b n d -> (b n) d")
    out_rows = out.rearrange("b n d -> (b n) d")

    with ExitStack() as ctx:
        def sb(name, shape, dt=F32):
            return ctx.enter_context(nc.sbuf_tensor(name, shape, dt))

        def bank(name):
            return ctx.enter_context(nc.psum_tensor(name, [P, 512], F32))

        def sem(name):
            return ctx.enter_context(nc.semaphore(name))

        w0 = sb("w0", [P, 2, C, F1 + 2], F32R)
        wq = sb("wq", [P, 2, C, D], F32R)
        wk = sb("wk", [P, 2, C, D], F32R)
        wv = sb("wv", [P, 2, C, D], F32R)
        wo = sb("wo", [P, 2, C, D], F32R)
        mask = sb("mask", [P, T, N], BF16)
        ident = sb("ident", [P, P])
        bo_wide = sb("bo_wide", [P, D])
        bq_col = sb("bq_col", [P, 4])
        bk_col = sb("bk_col", [P, 4])
        bv_col = sb("bv_col", [P, 4])
        minus_half = sb("minus_half", [P, T])
        gate_dve = sb("gate_dve", [P, 3 * T])
        zero = sb("zero", [P, 1])
        tokens = [sb(f"tokens{i}", [P, T, D]) for i in range(3)]
        turned = sb("turned", [P, 2, 2, C, P], F32R)
        h0 = sb("h0", [P, 2, T, F1], F32R)
        n_wide = sb("n_wide", [P, N])
        alpha = sb("alpha", [P, 2, N])
        terms = sb("terms", [P, T, 2])
        a_negmax = sb("a_negmax", [P, T])
        a_sum = sb("a_sum", [P, T])
        a_rsum = sb("a_rsum", [P, T])
        x1T = sb("x1T", [P, 2, C, N], F32R)
        q_st = sb("q_st", [P, 3, N], F32R)
        k_st = sb("k_st", [P, 3, 2, N], F32R)
        v_st = sb("v_st", [P, T, HEADS, 2 * DH], F32R)
        prob = sb("prob", [P, T, N])
        probT = sb("probT", [P, 2, 2, T, 2 * P], F32R)
        o_pair = sb("o_pair", [P, N])
        oT = sb("oT", [P, 2, C, N], F32R)
        negmax = sb("negmax", [P, T])
        psum_row = sb("psum_row", [P, T])
        rsum = sb("rsum", [P, T])
        stats = [sb(f"stats{i}", [P, T, 6]) for i in range(2)]
        meanvar = [sb(f"meanvar{i}", [P, T, 2]) for i in range(2)]
        var_eps = [sb(f"var_eps{i}", [P, T]) for i in range(2)]
        neg_mean = [sb(f"neg_mean{i}", [P, T]) for i in range(2)]
        rstd = [sb(f"rstd{i}", [P, T]) for i in range(2)]
        shift = [sb(f"shift{i}", [P, T]) for i in range(2)]

        S_bank = [bank(f"S_bank{i}") for i in range(2)]
        T_bank = [bank(f"T_bank{i}") for i in range(2)]
        O_bank = bank("O_bank")
        R_bank = [bank(f"R_bank{i}") for i in range(2)]
        L_bank = bank("L_bank")

        x_loaded = [sem(f"x_loaded{i}") for i in range(T)]
        y_stored = [sem(f"y_stored{i}") for i in range(T)]
        w_loaded = [sem(f"w_loaded{i}") for i in range(5)]
        adj_loaded, small_loaded = sem("adj_loaded"), sem("small_loaded")
        ident_built, mask_built = sem("ident_built"), sem("mask_built")
        w_hi, w_lo = sem("w_hi"), sem("w_lo")
        ring_mm, ring_done = sem("ring_mm"), sem("ring_done")
        solo_mm, solo_hi, solo_done = sem("solo_mm"), sem("solo_hi"), sem("solo_done")
        h_lo, terms_ready = sem("h_lo"), sem("terms_ready")
        nb_wide = sem("nb_wide")
        a_pre, a_leaky, a_red, a_exp, a_inv = (sem("a_pre"), sem("a_leaky"), sem("a_red"),
                                               sem("a_exp"), sem("a_inv"))
        x1_ready, bo_added = sem("x1_ready"), sem("bo_added")
        ln_dve = [sem(f"ln_dve{i}") for i in range(2)]
        ln_pool = [sem(f"ln_pool{i}") for i in range(2)]
        wa_done = sem("wa_done")
        qk_hi, qk_lo = sem("qk_hi"), sem("qk_lo")
        k_twice = [sem("k_twice_a"), sem("k_twice_b")]
        v_hi = sem("v_hi")
        s_mm, s_red, p_exp, p_inv, p_norm = (sem("s_mm"), sem("s_red"), sem("p_exp"),
                                             sem("p_inv"), sem("p_norm"))
        t_mm, t_hi = sem("t_mm"), sem("t_hi")
        t_lo = [sem(f"t_lo{i}") for i in range(2)]
        pv_mm = [sem(f"pv_mm{i}") for i in range(2)]
        o_lows, o_sum, o_hi, o_lo = sem("o_lows"), sem("o_sum"), sem("o_hi"), sem("o_lo")
        y_ready = sem("y_ready")

        SMALL = 6 * 16
        IDENT = 3
        start = Round(0, -2, FIRST_LAYER, last=False)
        prologue = Round(0, -1, FIRST_LAYER, last=False)
        end = Round(0, B, END, more=False, load=False)

        def pair_bank(R, kind, pair):
            if (kind, pair) == ("q", 1):
                return R_bank[1 - R.bank("k1")]
            return R_bank[R.bank(f"{kind}{pair}")]

        def solo_count(R, name, plus=1):
            n = R.n2 if name[0] in "AB" else R.nx
            return n(len(SOLO), SOLO.index(name) + plus)

        def all_rounds(eng, run):
            run(Round(0, 0, FIRST_ROUND, last=False))
            with eng.Fori(0, (B - 5) // 3) as i:
                for k in (1, 2, 3):
                    run(Round(i, k))
            run(Round(0, B - 4))
            run(Round(0, B - 3))
            run(Round(0, B - 2, load=False))
            run(Round(0, B - 1, LAST_ROUND, more=False, load=False))

        def w_stage():
            flat = prob[:, :, :].rearrange("p a b -> p (a b)")[:, 0:C * (F1 + 2)]
            return flat.rearrange("p (c f) -> p c f", c=C)

        def rows_of(h):
            return slice(DH * (h % 2), DH * (h % 2) + DH), slice(DH - DH * (h % 2), 2 * DH - DH * (h % 2))

        block = ctx.enter_context(nc.Block())

        @block.sync
        def _(sp):
            def load_tokens(R, i):
                if R.last:
                    sp.wait_ge(y_stored[i], R.n(16, 0))
                elif R.k == 0:
                    sp.wait_ge(w_lo, 4)
                sp.dma_start(tokens[R.buffer(2)][:, i, :], x_rows[R.rows(2, i), :]).then_inc(x_loaded[i], 16)

            def double_k(R, pair, which):
                h = 2 * pair + which
                own, other = rows_of(h)
                if which == 0:
                    sp.wait_ge(qk_lo, R.n(8, 2 * pair + 2))
                else:
                    sp.wait_ge(ring_done, R.ring(f"k{pair}", 1))
                sp.dma_start(k_st[other, R.slot(h), :, :].bitcast(F32),
                             k_st[own, R.slot(h), :, :].bitcast(F32)).then_inc(k_twice[which], 16)

            def extra(R, names):
                for kind, i in R.pieces(names):
                    if kind == "evA":
                        double_k(R, i, 0)
                    if kind == "evB":
                        double_k(R, i, 1)
                    if kind == "fin":
                        sp.wait_ge(y_ready, R.n(4, i - 3))
                        sp.dma_start(out_rows[R.rows(-1, i), :],
                                     tokens[R.buffer(-1)][:, i, :]).then_inc(y_stored[i], 16)
                    if kind == "ld":
                        load_tokens(R, i)

            def run_round(R):
                for h in range(HEADS):
                    for t in range(T):
                        extra(R, PLAN.get((h, t), []))

            for i in range(T):
                load_tokens(start, i)
            sp.dma_start(w_stage()[:, :, 0:F1], W.rearrange("(c p) f -> p c f", p=P)).then_inc(w_loaded[0], 16)
            for j in range(2):
                sp.dma_start(alpha[:, j, 0:F1], a[j, :, 0].partition_broadcast(P)).then_inc(small_loaded, 16)
            sp.dma_start(bo_wide[:, :], bo.partition_broadcast(P)).then_inc(small_loaded, 16)
            for dst, src in ((bq_col, bq), (bk_col, bk), (bv_col, bv)):
                sp.dma_start(dst[:, :], src).then_inc(small_loaded, 16)
            sp.dma_start(tokens[2][:, :, :].bitcast(I32), adj.rearrange("(t p) k -> p t k", p=P)).then_inc(adj_loaded, 16)
            for j, w in enumerate((WqT, WkT, WvT, WoT)):
                if j == 0:
                    sp.wait_ge(mask_built, 2)
                else:
                    sp.wait_ge(w_lo, j)
                stage = tokens[2] if j % 2 == 0 else prob
                sp.dma_start(stage[:, :, :], w.rearrange("(c p) n -> p c n", p=P)).then_inc(w_loaded[1 + j], 16)
            for i in range(T):
                load_tokens(prologue, i)
            extra(prologue, PROLOGUE)
            all_rounds(sp, run_round)
            extra(end, ENDING)
            for i in range(T):
                sp.wait_ge(y_stored[i], 16 * B)

        @block.tensor
        def _(pe):
            def ring(R, name):
                if due(R.ring(name, -1)):
                    pe.wait_ge(ring_done, R.ring(name, -1))
                return R_bank[R.bank(name)]

            def solo(R, name):
                if due(solo_count(R, name, 0)):
                    pe.wait_ge(solo_done, solo_count(R, name, 0))

            def solo_turn(src):
                for c in range(4):
                    last = pe.transpose(L_bank[:, c * P:(c + 1) * P], src[:, c * P:(c + 1) * P], ident[:, :])
                last.then_inc(solo_mm, 1)

            def project(dst, stationary, moving, done):
                todo = [(c, s, m) for c in range(C) for s, m in PARTS]
                for c, s, m in todo:
                    last = pe.matmul(dst, stationary(s, c), moving(m, c), start=(c, s, m) == todo[0],
                                     stop=(c, s, m) == todo[-1])
                last.then_inc(done, 1)

            def piece(R, kind, i):
                name = f"{kind}{i}"
                if kind == "A":
                    pe.wait_ge(x_loaded[i], R.n2(16, 16))
                    solo(R, name)
                    solo_turn(tokens[R.buffer(2)][:, i, :])
                if kind == "B":
                    solo(R, name)
                    project(L_bank[:, 0:F1 + 2], lambda s, c: turned[:, i % 2, s, c, :], lambda m, c: w0[:, m, c, :],
                            solo_mm)
                if kind == "N":
                    pe.wait_ge(nb_wide, R.nx(4, 4))
                    solo(R, kind)
                    solo_turn(n_wide[:, :])
                if kind == "C":
                    pe.wait_ge(a_exp, R.nx(4, i + 1))
                    solo(R, name)
                    solo_turn(alpha[:, i % 2, :])
                if kind == "D":
                    out_b = ring(R, name)
                    pe.wait_ge(solo_done, solo_count(R, f"C{i}"))
                    project(out_b[:, 0:F1], lambda s, c: turned[:, i % 2, s, c, :], lambda m, c: h0[:, m, c, :],
                            ring_mm)
                if kind == "E":
                    pe.wait_ge(x1_ready, R.nx(4, i + 1))
                    solo(R, name)
                    solo_turn(tokens[R.buffer(1)][:, i, :])
                if kind == "weights":
                    pe.wait_ge(w_lo, 5)
                if kind in ("q", "k"):
                    if name == "q4":
                        pe.wait_ge(solo_done, R.nx(len(SOLO), len(SOLO)))
                    c0, w = (i % 4) * P, wq if kind == "q" else wk
                    project(ring(R, name)[:, :], lambda s, c: w[:, s, c, c0:c0 + P], lambda m, c: x1T[:, m, c, :],
                            ring_mm)
                if kind in ("V", "W"):
                    if kind == "V":
                        pe.wait_ge(solo_done, solo_count(R, f"E{i}"))
                    c0 = 0 if kind == "V" else D // 2
                    project(ring(R, name)[:, 0:D // 2], lambda s, c: x1T[:, s, c, i * P:(i + 1) * P],
                            lambda m, c: wv[:, m, c, c0:c0 + D // 2], ring_mm)
                if kind == "O":
                    if i == 0:
                        pe.wait_ge(o_lo, R.n(4, 0))
                    project(ring(R, name)[:, :], lambda s, c: oT[:, s, c, i * P:(i + 1) * P],
                            lambda m, c: wo[:, m, c, :], ring_mm)
                if kind == "pv":
                    weigh(R, -1, 1)

            def scores(R, h, t):
                if t == 0:
                    pe.wait_ge(k_twice[h % 2], R.n(64, 16 * (h // 2 + 1)))
                if due(R.n(32, 4 * h + t - 1)):
                    pe.wait_ge(s_red, R.n(32, 4 * h + t - 1))
                for part in (HI, LO):
                    last = pe.matmul(S_bank[t % 2][:, :], q_st[:, R.slot(h), t * P:(t + 1) * P],
                                     k_st[:, R.slot(h), part, :], start=part == HI, stop=part == LO)
                last.then_inc(s_mm, 1)

            def turn_probs(R, h, t):
                pe.wait_ge(p_norm, R.n(32, 4 * h + t + 1))
                if due(R.n(16, 2 * h + t // 2)):
                    pe.wait_ge(t_lo[t % 2], R.n(16, 2 * h + t // 2))
                for c in range(T):
                    last = pe.transpose(T_bank[t % 2][:, c * P:(c + 1) * P], prob[:, t, c * P:(c + 1) * P],
                                        ident[:, :])
                last.then_inc(t_mm, 1)

            def weigh(R, h, half):
                for b in range(2):
                    pe.wait_ge(t_lo[b], R.n(16, 2 * h + half + 1))
                if half == 0 and h == 0:
                    pe.wait_ge(ring_done, R.ring("k1", -1))
                if half == 0 and h == HEADS // 2:
                    pe.wait_ge(ring_done, R.ring("W3", 1))
                if half == 0 and due(R.n(8, h)):
                    pe.wait_ge(o_sum, R.n(8, h))
                todo = [(c, s) for c in range(T) for s in (HI, LO)]
                for c, s in todo:
                    last = pe.matmul(O_bank[:, half * 2 * P:(half + 1) * 2 * P], v_st[:, c, h % HEADS, :],
                                     probT[:, half, s, c, :], start=(c, s) == todo[0], stop=(c, s) == todo[-1])
                last.then_inc(pv_mm[half], 1)

            def run_round(R):
                for h in range(HEADS):
                    for t in range(T):
                        turn_probs(R, h, t)
                        if h < HEADS - 1 or R.more:
                            scores(R, h + 1, t)
                        if t == 1 and h > 0:
                            weigh(R, h - 1, 1)
                        if t == 3:
                            weigh(R, h, 0)
                        for kind, i in R.pieces(PLAN.get((h, t), [])):
                            piece(R, kind, i)

            pe.wait_ge(ident_built, IDENT)
            for kind, i in start.pieces(START):
                if (kind, i) == ("B", 0):
                    pe.wait_ge(w_lo, 1)
                piece(start, kind, i)
            for kind, i in prologue.pieces(PROLOGUE):
                piece(prologue, kind, i)
            for t in range(T):
                scores(prologue, HEADS, t)
            all_rounds(pe, run_round)
            for kind, i in end.pieces(ENDING):
                piece(end, kind, i)

        @block.scalar
        def _(act):
            def split_hi(dst, src, done):
                act.activation(dst, src, ACT.Copy).then_inc(done, 1)

            def head_hi(R, pair, which):
                h = 2 * pair + which
                own, _ = rows_of(h)
                if due(R.n(32, 4 * (h - 2))):
                    act.wait_ge(s_mm, R.n(32, 4 * (h - 2)))
                for kind, b_col in (("q", bq_col), ("k", bk_col)):
                    ring_mm_value = R.ring("k1") if (kind, pair) == ("q", 1) else R.ring(f"{kind}{pair}", 1)
                    act.wait_ge(ring_mm, ring_mm_value)
                    dst = q_st[own, R.slot(h), :] if kind == "q" else k_st[own, R.slot(h), HI, :]
                    act.activation(dst, pair_bank(R, kind, pair)[own, :], ACT.Identity,
                                   bias=b_col[own, pair % 4:pair % 4 + 1]).then_inc(qk_hi, 1)

            def layer_apply(R, which, ahead, i, done):
                t_ap = tokens[R.buffer(ahead)][:, i, :]
                act.activation(t_ap, t_ap, ACT.Identity, bias=shift[which][:, i:i + 1],
                               scale=rstd[which][:, i:i + 1]).then_inc(done, 1)

            def piece(R, kind, i):
                name = f"{kind}{i}"
                if kind in ("A", "C"):
                    act.wait_ge(solo_mm, solo_count(R, name))
                    if name in ("A2", "A3"):
                        act.wait_ge(solo_mm, solo_count(R, f"B{i - 2}"))
                    if name in ("C2", "C3"):
                        act.wait_ge(ring_mm, R.ring(f"D{i - 2}", 1))
                    split_hi(turned[:, i % 2, HI, :, :], L_bank[:, :].rearrange("p (c t) -> p c t", c=C), solo_hi)
                if kind == "B":
                    act.wait_ge(solo_mm, solo_count(R, name))
                    split_hi(h0[:, HI, i, :], L_bank[:, 0:F1], solo_hi)
                if kind == "pre":
                    if i == 0:
                        act.wait_ge(solo_done, solo_count(R, "N"))
                    if i >= 2:
                        act.wait_ge(solo_mm, solo_count(R, f"C{i - 2}"))
                    act.activation(alpha[:, i % 2, :], n_wide[:, :], ACT.Identity,
                                   bias=terms[:, i, 0:1]).then_inc(a_pre, 1)
                if kind == "aexp":
                    act.wait_ge(a_red, R.nx(4, i + 1))
                    act.activation(alpha[:, i % 2, :], alpha[:, i % 2, :], ACT.Exp, bias=a_negmax[:, i:i + 1],
                                   scale=-1.0, accum_out=a_sum[:, i:i + 1]).then_inc(a_exp, 1)
                if kind == "lap":
                    act.wait_ge(ln_pool[0], R.nx(2, 2))
                    layer_apply(R, 0, 1, i, x1_ready)
                if kind == "E":
                    act.wait_ge(solo_mm, solo_count(R, name))
                    if i == 0 and not R.prologue:
                        act.wait_ge(ring_mm, R.ring("k3", 1))
                    split_hi(x1T[:, HI, :, i * P:(i + 1) * P], L_bank[:, :].rearrange("p (c t) -> p c t", c=C), solo_hi)
                if kind == "weights":
                    for j, w in enumerate((wq, wk, wv, wo)):
                        act.wait_ge(w_loaded[1 + j], 16)
                        stage = tokens[2] if j % 2 == 0 else prob
                        split_hi(w[:, HI, :, :], stage[:, :, :], w_hi)
                if kind == "evA":
                    head_hi(R, i, 0)
                if kind == "evB":
                    head_hi(R, i, 1)
                if kind in ("evV", "evW"):
                    v, h0_ = kind[-1], 0 if kind == "evV" else HEADS // 2
                    act.wait_ge(ring_mm, R.ring(f"{v}{i}", 1))
                    if i == 0:
                        if due(R.n(8, h0_ or 0)) and not R.prologue:
                            act.wait_ge(pv_mm[1], R.n(8, 4) if kind == "evV" else R.n(8, 0))
                    split_hi(v_st[:, i, h0_:h0_ + HEADS // 2, 0:DH],
                             R_bank[R.bank(f"{v}{i}")][:, 0:D // 2].rearrange("p (h d) -> p h d", d=DH), v_hi)
                if kind == "pv":
                    head_lows(R, -1)
                    pair_hi(R, -1)
                if kind == "fin":
                    act.wait_ge(ln_pool[1], R.n(2, 0))
                    layer_apply(R, 1, -1, i, y_ready)

            def exps(R, h, t):
                act.wait_ge(s_red, R.n(32, 4 * h + t + 1))
                act.activation(prob[:, t, :], prob[:, t, :], ACT.Exp, bias=negmax[:, t:t + 1], scale=-1.0,
                               accum_out=psum_row[:, t:t + 1]).then_inc(p_exp, 1)

            def probs_hi(R, h, t):
                if due(R.n(8, h)):
                    act.wait_ge(pv_mm[t // 2], R.n(8, h))
                act.wait_ge(t_mm, R.n(32, 4 * h + t + 1))
                split_hi(probT[:, t // 2, HI, :, (t % 2) * P:(t % 2 + 1) * P],
                         T_bank[t % 2][:, :].rearrange("p (c q) -> p c q", c=T), t_hi)

            def head_lows(R, h):
                own, _ = rows_of(h)
                if due(R.n(4, h // 2)):
                    act.wait_ge(o_lo, R.n(4, h // 2))
                act.wait_ge(pv_mm[1], R.n(8, h + 1))
                act.activation(o_pair[own, :], O_bank[DH:2 * DH, :], ACT.Identity,
                               bias=bv_col[own, h // 2 % 4:h // 2 % 4 + 1]).then_inc(o_lows, 1)

            def pair_hi(R, pair):
                if pair == 0 and R.last:
                    act.wait_ge(ring_mm, R.ring("O3", 1))
                act.wait_ge(o_sum, R.n(8, 2 * pair + 2))
                split_hi(oT[:, HI, pair % 4, :], o_pair[:, :], o_hi)

            def run_round(R):
                for h in range(HEADS):
                    for t in range(T):
                        probs_hi(R, h, t)
                        if h < HEADS - 1 or R.more:
                            exps(R, h + 1, t)
                        if t == 1 and h > 0:
                            head_lows(R, h - 1)
                        if t == 2 and h > 0 and h % 2 == 0:
                            pair_hi(R, h // 2 - 1)
                        for kind, i in R.pieces(PLAN.get((h, t), [])):
                            piece(R, kind, i)

            act.wait_ge(w_loaded[0], 16)
            act.wait_ge(wa_done, 2 * C)
            split_hi(w0[:, HI, :, :], w_stage(), w_hi)
            act.wait_ge(small_loaded, SMALL)
            for R, pieces in ((start, START), (prologue, PROLOGUE)):
                for kind, i in R.pieces(pieces):
                    piece(R, kind, i)
            for t in range(T):
                exps(prologue, HEADS, t)
            all_rounds(act, run_round)
            for kind, i in end.pieces(ENDING):
                piece(end, kind, i)

        @block.vector
        def _(dve):
            def gate(i):
                dve.memset(gate_dve[:, i:i + 1], 0.0)

            def split_lo(dst, src, hi, done):
                dve.tensor_tensor(dst, src, hi.bitcast(F32), ALU.subtract).then_inc(done, 1)

            def layer_stats(which, count, i, t_ap):
                dve.bn_stats(stats[which][:, i, :], t_ap).then_inc(ln_dve[which], 1)
                dve.wait_ge(ln_dve[which], count(2 * i + 1))
                gate(which * T + i)
                dve.bn_aggr(meanvar[which][:, i, :], stats[which][:, i, :]).then_inc(ln_dve[which], 1)

            def layer_scales(which, count):
                dve.wait_ge(ln_dve[which], count(2 * T))
                dve.tensor_scalar(var_eps[which][:, :], meanvar[which][:, :, 1], EPS, None,
                                  ALU.add).then_inc(ln_dve[which], 1)
                dve.tensor_scalar(neg_mean[which][:, :], meanvar[which][:, :, 0], -1.0, None,
                                  ALU.mult).then_inc(ln_dve[which], 1)

            def head_lo(R, pair, which):
                h = 2 * pair + which
                own, other = rows_of(h)
                for j, (kind, b_col) in enumerate((("q", bq_col), ("k", bk_col))):
                    dve.wait_ge(qk_hi, R.n(16, 4 * pair + 2 * which + j + 1))
                    hi, dst = ((q_st[own, R.slot(h), :], q_st[other, R.slot(h), :]) if kind == "q" else
                               (k_st[own, R.slot(h), HI, :], k_st[own, R.slot(h), LO, :]))
                    dve.scalar_tensor_tensor(out=dst, in0=pair_bank(R, kind, pair)[own, :],
                                             scalar=b_col[own, pair % 4:pair % 4 + 1], in1=hi.bitcast(F32),
                                             op0=ALU.add, op1=ALU.subtract).then_inc(qk_lo if which == 0 else ring_done, 1)

            def solo_hi_count(R, name):
                n = R.n2 if name[0] in "AB" else R.nx
                return n(len(SOLO) - 1, len([u for u in SOLO[:SOLO.index(name) + 1] if u != "N"]))

            def piece(R, kind, i):
                name = f"{kind}{i}"
                if kind in ("A", "C"):
                    if kind == "C":
                        dve.wait_ge(a_exp, R.nx(4, i + 1))
                        dve.reciprocal(a_rsum[:, i:i + 1], a_sum[:, i:i + 1]).then_inc(a_inv, 1)
                    dve.wait_ge(solo_hi, solo_hi_count(R, name))
                    split_lo(turned[:, i % 2, LO, :, :], L_bank[:, :].rearrange("p (c t) -> p c t", c=C),
                             turned[:, i % 2, HI, :, :], solo_done)
                if kind == "B":
                    dve.wait_ge(solo_hi, solo_hi_count(R, name))
                    split_lo(h0[:, LO, i, :], L_bank[:, 0:F1], h0[:, HI, i, :], h_lo)
                    dve.tensor_copy(terms[:, i, :], L_bank[:, F1:F1 + 2]).then_inc(terms_ready, 1)
                    t_ap = tokens[R.buffer(2)][:, i, F1:D]
                    dve.tensor_tensor(t_ap, L_bank[:, 0:F1], t_ap, ALU.add).then_inc(solo_done, 1)
                if kind == "N":
                    dve.wait_ge(solo_mm, solo_count(R, "N"))
                    dve.tensor_copy(n_wide[:, :], L_bank[:, :]).then_inc(solo_done, 1)
                if kind == "red":
                    al = alpha[:, i % 2, :]
                    dve.wait_ge(a_pre, R.nx(4, i + 1))
                    dve.scalar_tensor_tensor(out=al, in0=al, scalar=LEAK, in1=al, op0=ALU.mult,
                                             op1=ALU.max).then_inc(a_leaky, 1)
                    dve.wait_ge(a_leaky, R.nx(4, i + 1))
                    gate(2 * T + i)
                    dve.tensor_tensor_reduce(al, al, mask[:, i, :], -1.0, HUGE, ALU.add, ALU.min,
                                             a_negmax[:, i:i + 1]).then_inc(a_red, 1)
                if kind == "evD":
                    out_name, t_ap = f"D{i}", tokens[R.buffer(1)][:, i, 0:F1]
                    dve.wait_ge(a_inv, R.nx(4, i + 1))
                    dve.wait_ge(ring_mm, R.ring(out_name, 1))
                    dve.scalar_tensor_tensor(out=t_ap, in0=R_bank[R.bank(out_name)][:, 0:F1],
                                             scalar=a_rsum[:, i:i + 1], in1=t_ap, op0=ALU.mult,
                                             op1=ALU.add).then_inc(ring_done, 1)
                if kind == "lst":
                    dve.wait_ge(ring_done, R.ring(f"D{i}", 1))
                    layer_stats(0, lambda c: R.nx(10, c), i, tokens[R.buffer(1)][:, i, :])
                if kind == "lrs":
                    layer_scales(0, lambda c: R.nx(10, c))
                if kind == "E":
                    dve.wait_ge(solo_hi, solo_hi_count(R, name))
                    split_lo(x1T[:, LO, :, i * P:(i + 1) * P], L_bank[:, :].rearrange("p (c t) -> p c t", c=C),
                             x1T[:, HI, :, i * P:(i + 1) * P], solo_done)
                if kind == "weights":
                    for j, w in enumerate((wq, wk, wv, wo)):
                        dve.wait_ge(w_hi, 2 + j)
                        stage = tokens[2] if j % 2 == 0 else prob
                        split_lo(w[:, LO, :, :], stage[:, :, :], w[:, HI, :, :], w_lo)
                if kind == "evA":
                    head_lo(R, i, 0)
                if kind == "evB":
                    head_lo(R, i, 1)
                if kind in ("evV", "evW"):
                    v, h0_ = kind[-1], 0 if kind == "evV" else HEADS // 2
                    dve.wait_ge(v_hi, R.n(8, 4 + i + 1) if kind == "evW" else R.nx(8, i + 1))
                    split_lo(v_st[:, i, h0_:h0_ + HEADS // 2, DH:2 * DH],
                             R_bank[R.bank(f"{v}{i}")][:, 0:D // 2].rearrange("p (h d) -> p h d", d=DH),
                             v_st[:, i, h0_:h0_ + HEADS // 2, 0:DH], ring_done)
                if kind == "pv":
                    head_sum(R, -1)
                if kind == "evO":
                    out_name, t_ap = f"O{i}", tokens[R.buffer(-1)][:, i, :]
                    dve.wait_ge(bo_added, R.n(4, i - 3))
                    dve.wait_ge(ring_mm, R.ring(out_name, 1))
                    dve.tensor_tensor(t_ap, R_bank[R.bank(out_name)][:, :], t_ap, ALU.add).then_inc(ring_done, 1)
                if kind == "yst":
                    dve.wait_ge(ring_done, R.ring(f"O{i}", 1))
                    layer_stats(1, lambda c: R.n(10, c - 10), i, tokens[R.buffer(-1)][:, i, :])
                if kind == "yrs":
                    layer_scales(1, lambda c: R.n(10, c - 10))

            def reduce_scores(R, h, t, unit_before=None):
                if due(R.n(32, 4 * (h - 1) + t + 1)) and not R.prologue:
                    dve.wait_ge(t_mm, R.n(32, 4 * (h - 1) + t + 1))
                dve.wait_ge(s_mm, R.n(32, 4 * h + t + 1))
                if unit_before is not None:
                    invert_sums(R, *unit_before)
                dve.tensor_tensor_reduce(prob[:, t, :], S_bank[t % 2][:, :], mask[:, t, :], -SCALE, HUGE, ALU.add,
                                         ALU.min, negmax[:, t:t + 1]).then_inc(s_red, 1)

            def invert_sums(R, h, t):
                dve.wait_ge(p_exp, R.n(32, 4 * h + t + 1))
                dve.reciprocal(rsum[:, t:t + 1], psum_row[:, t:t + 1]).then_inc(p_inv, 1)

            def probs_lo(R, h, t):
                dve.wait_ge(t_hi, R.n(32, 4 * h + t + 1))
                cols = slice((t % 2) * P, (t % 2 + 1) * P)
                split_lo(probT[:, t // 2, LO, :, cols], T_bank[t % 2][:, :].rearrange("p (c q) -> p c q", c=T),
                         probT[:, t // 2, HI, :, cols], t_lo[t % 2])

            def head_sum(R, h):
                own, _ = rows_of(h)
                dve.wait_ge(o_lows, R.n(8, h + 1))
                dve.tensor_tensor(o_pair[own, :], O_bank[0:DH, :], o_pair[own, :], ALU.add).then_inc(o_sum, 1)

            def run_round(R):
                for h in range(HEADS):
                    for t in range(T):
                        probs_lo(R, h, t)
                        before = (h + 1, t - 1) if t > 0 else (h, T - 1) if h > 0 or R.last else None
                        if h < HEADS - 1 or R.more:
                            reduce_scores(R, h + 1, t, before)
                        elif t == 0:
                            invert_sums(R, *before)
                        if t == 1 and h > 0:
                            head_sum(R, h - 1)
                        for kind, i in R.pieces(PLAN.get((h, t), [])):
                            piece(R, kind, i)

            dve.memset(minus_half[:, :], -0.5).then_inc(mask_built, 1)
            dve.wait_ge(adj_loaded, 16)
            dve.tensor_scalar(mask[:, :, :], tokens[2][:, :, :].bitcast(I32), 0.0, MASKED, ALU.is_equal,
                              ALU.mult).then_inc(mask_built, 1)
            dve.wait_ge(w_loaded[0], 16)
            dve.wait_ge(small_loaded, SMALL)
            for j in range(2):
                for c in range(C):
                    if j + c > 0:
                        dve.wait_ge(wa_done, j * C + c)
                    dve.tensor_tensor_reduce(n_wide[:, 0:F1], w_stage()[:, c, 0:F1], alpha[:, j, 0:F1], 1.0, 0.0,
                                             ALU.mult, ALU.add, w_stage()[:, c, F1 + j:F1 + j + 1]).then_inc(wa_done, 1)
            dve.wait_ge(w_hi, 1)
            split_lo(w0[:, LO, :, :], w_stage(), w0[:, HI, :, :], w_lo)
            for R, pieces in ((start, START), (prologue, PROLOGUE)):
                for kind, i in R.pieces(pieces):
                    piece(R, kind, i)
            for t in range(T):
                reduce_scores(prologue, HEADS, t)
                invert_sums(prologue, HEADS, t)
            all_rounds(dve, run_round)
            for kind, i in end.pieces(ENDING):
                piece(end, kind, i)

        @block.gpsimd
        def _(pool):
            def normalise(R, h, t):
                pool.wait_ge(p_inv, R.n(32, 4 * h + t + 1))
                pool.tensor_tensor(prob[:, t, :], prob[:, t, :], rsum[:, t:t + 1].to_broadcast([P, N]),
                                   ALU.mult).then_inc(p_norm, 1)

            def scales(which, full, half):
                pool.wait_ge(ln_dve[which], full)
                pool.tensor_tensor(rstd[which][:, :], var_eps[which][:, :], minus_half[:, :],
                                   ALU.pow).then_inc(ln_pool[which], 1)
                pool.wait_ge(ln_pool[which], half)
                pool.tensor_tensor(shift[which][:, :], neg_mean[which][:, :], rstd[which][:, :],
                                   ALU.mult).then_inc(ln_pool[which], 1)

            def pair_lo(R, pair):
                pool.wait_ge(o_hi, R.n(4, pair + 1))
                pool.tensor_tensor(oT[:, LO, pair % 4, :], o_pair[:, :], oT[:, HI, pair % 4, :].bitcast(F32),
                                   ALU.subtract).then_inc(o_lo, 1)

            def piece(R, kind, i):
                if kind == "nbm":
                    pool.wait_ge(terms_ready, R.n2(4, 4))
                    for j in range(T):
                        pool.tensor_tensor(n_wide[:, j * P:(j + 1) * P], terms[:, j, 1:2].to_broadcast([P, P]),
                                           zero[:, :].to_broadcast([P, P]), ALU.add).then_inc(nb_wide, 1)
                if kind == "lrs":
                    scales(0, R.nx(10, 10), R.nx(2, 1))
                if kind == "yrs":
                    scales(1, R.n(10, 0), R.n(2, -1))
                if kind == "bo":
                    pool.wait_ge(solo_mm, solo_count(R, f"E{i}"))
                    t_ap = tokens[R.buffer(1)][:, i, :]
                    pool.tensor_tensor(t_ap, t_ap, bo_wide[:, :], ALU.add).then_inc(bo_added, 1)
                if kind == "pv":
                    pair_lo(R, -1)

            def run_round(R):
                for h in range(HEADS):
                    for t in range(T):
                        if t > 0 and (h < HEADS - 1 or R.more):
                            normalise(R, h + 1, t - 1)
                        if t == 0 and (h > 0 or R.last):
                            normalise(R, h, T - 1)
                        if t == 2 and h > 0 and h % 2 == 0:
                            pair_lo(R, h // 2 - 1)
                        for kind, i in R.pieces(PLAN.get((h, t), [])):
                            piece(R, kind, i)

            pool.memset(zero[:, :], 0.0).then_inc(ident_built, 1)
            pool.memset(ident[:, :], 0.0).then_inc(ident_built, 1)
            pool.wait_ge(ident_built, 2)
            pool.affine_select(out=ident[:, :], in_=ident[:, :], compare_op=ALU.not_equal, fill=1.0, base=0,
                               pattern=[[-1, P]], channel_multiplier=1).then_inc(ident_built, 1)
            pool.wait_ge(small_loaded, SMALL)
            pool.wait_ge(mask_built, 1)
            for R, pieces in ((start, START), (prologue, PROLOGUE)):
                for kind, i in R.pieces(pieces):
                    piece(R, kind, i)
            for t in range(T):
                normalise(prologue, HEADS, t)
            all_rounds(pool, run_round)
            for kind, i in end.pieces(ENDING):
                piece(end, kind, i)


def kernel(x, adj, L0_gnn_W, L0_gnn_a, L1_gnn_Wq, L1_gnn_bq, L1_gnn_Wk, L1_gnn_bk, L1_gnn_Wv, L1_gnn_bv,
           L1_gnn_Wo, L1_gnn_bo):
    import numpy as np
    import concourse.bacc as bacc
    from concourse.bass_utils import run_bass_kernel_spmd

    def columns(b):
        return np.ascontiguousarray(np.asarray(b).reshape(-1, P).T)

    def turned(w):
        return np.ascontiguousarray(np.asarray(w).T)

    arrays = {
        "x": np.ascontiguousarray(x), "adj": np.ascontiguousarray(adj), "W": np.ascontiguousarray(L0_gnn_W),
        "a": np.ascontiguousarray(L0_gnn_a), "WqT": turned(L1_gnn_Wq), "bq": columns(L1_gnn_bq),
        "WkT": turned(L1_gnn_Wk), "bk": columns(L1_gnn_bk), "WvT": turned(L1_gnn_Wv), "bv": columns(L1_gnn_bv),
        "WoT": turned(L1_gnn_Wo), "bo": np.ascontiguousarray(L1_gnn_bo),
    }
    nc = bacc.Bacc("TRN2", target_bir_lowering=False, num_devices=1, dynamic_dma_scratch_size=1024)
    args = [nc.dram_tensor(name, v.shape, mybir.dt.from_np(v.dtype), kind="ExternalInput").ap()
            for name, v in arrays.items()]
    out = nc.dram_tensor("out", arrays["x"].shape, F32, kind="ExternalOutput").ap()
    graph_layers(nc, *args, out)
    r = run_bass_kernel_spmd(nc, [arrays], core_ids=[0])
    return r.results[0]["out"]
```

```python
from contextlib import ExitStack

import concourse.bass as bass
from concourse import mybir

ALU = mybir.AluOpType
ACT = mybir.ActivationFunctionType
F32 = mybir.dt.float32
F32R = mybir.dt.float32r
BF16 = mybir.dt.bfloat16
I32 = mybir.dt.int32

P = 128
HEADS = 8
EPS = 1e-5
LEAK = 0.2
MASKED = -3.0e38
HUGE = 3.0e38
HI, LO = 0, 1
PARTS = ((HI, HI), (HI, LO), (LO, HI))

TENSOR_PLAN = (
    "turn scores N",
    "turn k1 scores pv",
    "scores turn",
    "scores turn O0 weighA",
    "turn C0 scores O1",
    "turn scores weighB O2",
    "turn scores O3",
    "C1 turn weighA scores",
    "turn scores q2",
    "turn weighB scores k2",
    "scores turn",
    "weighA scores turn",
    "D0 D1 C2 turn W0 scores",
    "W1 turn scores weighB C3 W2 W3",
    "turn scores D2 D3",
    "scores turn weighA q3",
    "turn scores",
    "turn k3 weighB scores",
    "scores turn E0",
    "scores turn E1 weighA",
    "turn V0 scores",
    "E2 weighB turn scores",
    "E3 V1 turn scores",
    "turn weighA scores A0 q4 B0",
    "scores turn A1 k4",
    "weighB turn scores",
    "B1 turn scores",
    "V2 A2 turn scores weighA B2",
    "turn scores V3",
    "A3 turn scores weighB",
    "scores turn",
    "B3 q1 turn scores weighA",
)
SCALAR_PLAN = (
    "hi exp evQ1",
    "hi pv exp pre0",
    "hi pre1 exp",
    "aexp0 exp hi",
    "hi exp",
    "hi lows C0 exp",
    "aexp1 hi pre2 C1 exp",
    "hi exp pre3",
    "hi exp",
    "hi lows evQ2 exp aexp2",
    "pair hi exp aexp3",
    "fin0 hi exp evW0",
    "C2 hi fin1 evW1 exp",
    "hi lows C3 fin2 evW2 exp",
    "hi evW3 fin3 exp",
    "hi exp",
    "hi exp",
    "hi evQ3 lap0 lows exp",
    "hi E0 lap1 pair exp",
    "hi lap2 E1 exp evV0 lap3",
    "E2 hi exp",
    "hi lows E3 exp evV1",
    "hi A0 exp",
    "hi B0 exp",
    "hi A1 exp evQ4",
    "hi lows exp B1",
    "hi pair A2 exp evV2",
    "hi B2 exp A3",
    "hi exp evV3",
    "exp hi lows",
    "B3 hi exp",
    "hi exp",
)
VECTOR_PLAN = (
    "reduce lo N",
    "reduce lo pv evQ1",
    "reduce red0 lo",
    "reduce lo",
    "evO0 lo reduce red1",
    "lo yst0 reduce evO1 sum evO2",
    "C0 reduce lo yst1 evO3 C1",
    "yst2 reduce lo red2",
    "lo reduce red3 yst3",
    "yrs sum lo reduce evQ2",
    "reduce lo",
    "evD0 lst0 reduce lo evD1",
    "reduce lo evW0 C2 evW1",
    "lo reduce sum evW2 lst1 C3 evW3",
    "lo evD2 evD3 reduce lst2",
    "reduce lo",
    "reduce lst3 lo lrs",
    "evQ3 reduce sum lo",
    "E0 reduce lo",
    "reduce lo E1",
    "reduce E2 lo",
    "evV0 lo reduce sum E3",
    "reduce evV1 A0 lo",
    "reduce lo B0",
    "reduce A1 lo evQ4",
    "reduce sum B1 lo",
    "reduce lo A2",
    "reduce evV2 B2 lo",
    "reduce A3 lo",
    "reduce lo sum",
    "reduce lo",
    "B3 reduce lo evV3",
)
GPSIMD_PLAN = (
    "norm",
    "pv norm",
    "norm",
    "norm",
    "norm",
    "norm",
    "norm",
    "norm",
    "yrs norm",
    "norm",
    "norm pair",
    "norm",
    "norm",
    "norm",
    "norm",
    "norm",
    "norm",
    "lrs norm bo0",
    "norm pair",
    "norm bo1 bo2",
    "norm",
    "norm bo3",
    "norm",
    "norm",
    "norm",
    "norm",
    "norm pair",
    "norm",
    "norm",
    "norm",
    "norm nbm",
    "norm",
)
SP_PLAN = (
    "cpA1",
    "",
    "",
    "",
    "cpB1",
    "",
    "",
    "",
    "",
    "",
    "",
    "cpA2 fin0 cpB2",
    "fin1 fin2",
    "",
    "ld0 ld1",
    "",
    "",
    "",
    "ld2 fin3",
    "ld3",
    "cpA3",
    "",
    "",
    "",
    "cpB3",
    "",
    "cpA4 cpB4",
    "",
    "",
    "",
    "",
    "",
)
START = "A0 A1 B0 w0 A2 B1 w1 A3 B2 B3 nbm"
PROLOGUE = """N pre0 pre1 red0 red1 aexp0 aexp1 C0 C1 pre2 red2 D0 D1 pre3 red3 evD0 evD1 aexp2 lst0 C2 aexp3 C3 lst1
              D2 D3 evD2 lst2 evD3 lst3 lrs A0 w2 A1 lap0 lap1 lap2 B0 lap3 A2 E0 E1 E2 V0 E3 evV0 A3 V1 evV1 B1 evQ4
              q4 cpA4 k4 bo0 B2 V2 V3 evV2 bo1 bo2 cpB4 bo3 w3 B3 evV3 q1 nbm"""
ENDING = "pv O0 O1 evO0 O2 yst0 evO1 yst1 O3 evO2 yst2 evO3 yst3 yrs fin0 fin1 fin2 fin3"
SECOND_ONLY = set("AB") | {"nbm", "ld"}
NEXT_ONLY = set("NCDEV") | {"pre", "red", "aexp", "evD", "lst", "lrs", "lap", "bo", "evV"}
LAST_ONLY = {"pv", "O", "evO", "yst", "yrs", "fin"}


def parse(name):
    return (name[:-1], int(name[-1])) if name[-1].isdigit() else (name, 0)


def ring_uses(plan):
    return [name for name in " ".join(plan).split() if parse(name)[0] in ("q", "k", "V", "W", "O", "D")]


FIRST_LAYER = ring_uses([PROLOGUE])
ROUND = ring_uses(TENSOR_PLAN)
assert ROUND[0] == "k1" and ROUND[-1] == "q1"
assert all(f"evQ{p}" in " ".join(VECTOR_PLAN[8 * p - 8:]) for p in (1, 2, 3, 4))
FIRST_ROUND = [u for u in ROUND if u[0] != "O"]
LAST_ROUND = [u for u in ROUND if u[0] in "kOqW" and u not in ("q1", "q4", "k4")]
END = ring_uses([ENDING])
RING0 = len(FIRST_LAYER) + len(FIRST_ROUND) - len(ROUND)
SOLO = ["A0", "B0", "A1", "B1", "A2", "B2", "A3", "B3", "N", "C0", "C1", "C2", "C3", "E0", "E1", "E2", "E3"]
FIRST_SOLO = [name for name in START.split() if name in SOLO] + [name for name in PROLOGUE.split() if name in SOLO]


class Round:

    def __init__(self, i, k, uses=ROUND, last=True, more=True, load=True):
        self.i, self.k, self.uses = i, k, uses
        self.last, self.more, self.load = last, more, load
        self.prologue = uses is FIRST_LAYER
        self.ring0 = {id(FIRST_LAYER): len(ROUND), id(FIRST_ROUND): len(FIRST_LAYER),
                      id(END): RING0 + len(LAST_ROUND) - len(ROUND)}.get(id(uses), RING0)

    def n(self, per_graph, extra):
        return self.i * (3 * per_graph) + (self.k * per_graph + extra)

    def nx(self, per_graph, extra):
        return self.n(per_graph, per_graph + extra)

    def n2(self, per_graph, extra):
        return self.n(per_graph, 2 * per_graph + extra)

    def ring(self, name, extra=0):
        return self.n(len(ROUND), self.ring0 + self.uses.index(name) + extra)

    def bank(self, name):
        return (self.ring0 + self.uses.index(name)) % 2

    def buffer(self, ahead):
        return (self.k + ahead) % 3

    def rows(self, ahead, tile):
        first = self.n(512, 512 * ahead + P * tile)
        return slice(first, first + P) if isinstance(first, int) else bass.ds(first, P)

    def pieces(self, names):
        for name in names.split():
            kind, index = parse(name)
            ahead = kind in NEXT_ONLY or kind in ("q", "k", "evQ", "cpA", "cpB") and index == 4 or name == "q1"
            if ((self.more or not ahead) and (self.last or kind not in LAST_ONLY)
                    and (self.load or kind not in SECOND_ONLY)):
                yield kind, index


def due(value):
    return not isinstance(value, int) or value > 0


def graph_layers(nc, x, adj, W, a, WqT, bq, WkT, bk, WvT, bv, WoT, bo, out):
    B, N, D = x.shape
    F1 = W.shape[1]
    T = N // P
    C = D // P
    DH = D // HEADS
    SCALE = float(DH) ** -0.5
    assert N == 512 and D == 512 and F1 == 256 and T == 4 and DH == 64 and B % 3 == 2 and B >= 8
    x_rows = x.rearrange("b n d -> (b n) d")
    out_rows = out.rearrange("b n d -> (b n) d")

    with ExitStack() as ctx:
        def sb(name, shape, dt=F32):
            return ctx.enter_context(nc.sbuf_tensor(name, shape, dt))

        def bank(name):
            return ctx.enter_context(nc.psum_tensor(name, [P, 512], F32))

        def sem(name):
            return ctx.enter_context(nc.semaphore(name))

        w0 = sb("w0", [P, 2, C, F1 + 2], F32R)
        wq = sb("wq", [P, 2, C, D], F32R)
        wk = sb("wk", [P, 2, C, D], F32R)
        wv = sb("wv", [P, 2, C, D], F32R)
        wo = sb("wo", [P, 2, C, D], F32R)
        mask = sb("mask", [P, T, N], BF16)
        ident = sb("ident", [P, P])
        bo_wide = sb("bo_wide", [P, D])
        bq_col = sb("bq_col", [P, 4])
        bk_col = sb("bk_col", [P, 4])
        bv_col = sb("bv_col", [P, 4])
        minus_half = sb("minus_half", [P, T])
        gate_dve = sb("gate_dve", [P, 3 * T])
        zero = sb("zero", [P, 1])
        tokens = [sb(f"tokens{i}", [P, T, D]) for i in range(3)]
        turned = sb("turned", [P, 2, 2, C, P], F32R)
        h0 = sb("h0", [P, 2, T, F1], F32R)
        n_wide = sb("n_wide", [P, N])
        alpha = sb("alpha", [P, 2, N])
        terms = sb("terms", [P, T, 2])
        a_negmax = sb("a_negmax", [P, T])
        a_sum = sb("a_sum", [P, T])
        a_rsum = sb("a_rsum", [P, T])
        x1T = sb("x1T", [P, 2, C, N], F32R)
        q_pair = sb("q_pair", [P, 2, N], F32R)
        k_pair = sb("k_pair", [P, 2, N], F32R)
        q_st = sb("q_st", [P, 2, N], F32R)
        k_st = sb("k_st", [P, 2, 2, N], F32R)
        v_st = sb("v_st", [P, T, HEADS, 2 * DH], F32R)
        prob = sb("prob", [P, T, N])
        probT = sb("probT", [P, 2, 2, T, 2 * P], F32R)
        o_pair = sb("o_pair", [P, N])
        oT = sb("oT", [P, 2, C, N], F32R)
        negmax = sb("negmax", [P, T])
        psum_row = sb("psum_row", [P, T])
        rsum = sb("rsum", [P, T])
        stats = [sb(f"stats{i}", [P, T, 6]) for i in range(2)]
        meanvar = [sb(f"meanvar{i}", [P, T, 2]) for i in range(2)]
        var_eps = [sb(f"var_eps{i}", [P, T]) for i in range(2)]
        neg_mean = [sb(f"neg_mean{i}", [P, T]) for i in range(2)]
        rstd = [sb(f"rstd{i}", [P, T]) for i in range(2)]
        shift = [sb(f"shift{i}", [P, T]) for i in range(2)]

        S_bank = [bank(f"S_bank{i}") for i in range(2)]
        T_bank = [bank(f"T_bank{i}") for i in range(2)]
        O_bank = bank("O_bank")
        R_bank = [bank(f"R_bank{i}") for i in range(2)]
        L_bank = bank("L_bank")

        x_loaded = [sem(f"x_loaded{i}") for i in range(T)]
        y_stored = [sem(f"y_stored{i}") for i in range(T)]
        w_loaded = [sem(f"w_loaded{i}") for i in range(5)]
        adj_loaded, a_loaded, small_loaded = sem("adj_loaded"), sem("a_loaded"), sem("small_loaded")
        ident_built, mask_built = sem("ident_built"), sem("mask_built")
        w_hi, w_lo = sem("w_hi"), sem("w_lo")
        ring_mm, ring_done = sem("ring_mm"), sem("ring_done")
        solo_mm, solo_hi, solo_done = sem("solo_mm"), sem("solo_hi"), sem("solo_done")
        h_lo, terms_ready = sem("h_lo"), sem("terms_ready")
        nb_wide = sem("nb_wide")
        a_pre, a_leaky, a_red, a_exp, a_inv = (sem("a_pre"), sem("a_leaky"), sem("a_red"),
                                               sem("a_exp"), sem("a_inv"))
        x1_ready, bo_added = sem("x1_ready"), sem("bo_added")
        ln_dve = [sem(f"ln_dve{i}") for i in range(2)]
        ln_pool = [sem(f"ln_pool{i}") for i in range(2)]
        wa_done = sem("wa_done")
        qk_hi = sem("qk_hi")
        head_copied = [sem("head_copied_a"), sem("head_copied_b")]
        v_hi = sem("v_hi")
        s_mm, s_red, p_exp, p_inv, p_norm = (sem("s_mm"), sem("s_red"), sem("p_exp"),
                                             sem("p_inv"), sem("p_norm"))
        t_mm, t_hi = sem("t_mm"), sem("t_hi")
        t_lo = [sem(f"t_lo{i}") for i in range(2)]
        pv_mm = [sem(f"pv_mm{i}") for i in range(2)]
        o_lows, o_sum, o_hi, o_lo = sem("o_lows"), sem("o_sum"), sem("o_hi"), sem("o_lo")
        y_ready = sem("y_ready")

        SMALL = 4 * 16
        IDENT = 3
        start = Round(0, -2, FIRST_LAYER, last=False)
        prologue = Round(0, -1, FIRST_LAYER, last=False)
        end = Round(0, B, END, more=False, load=False)

        def pair_bank(R, kind, pair):
            if (kind, pair) == ("q", 1):
                return R_bank[1 - R.bank("k1")]
            return R_bank[R.bank(f"{kind}{pair}")]

        def solo_count(R, name, plus=1):
            if R.prologue:
                return first_solo(R, name) + plus
            n = R.n2 if name[0] in "AB" else R.nx
            return n(len(SOLO), SOLO.index(name) + plus)

        def first_solo(R, name):
            return FIRST_SOLO.index(name, 0 if R is start else 8)

        def solo_bank(R, name):
            return O_bank if R.prologue and first_solo(R, name) % 2 else L_bank

        def all_rounds(eng, run):
            run(Round(0, 0, FIRST_ROUND, last=False))
            with eng.Fori(0, (B - 5) // 3) as i:
                for k in (1, 2, 3):
                    run(Round(i, k))
            run(Round(0, B - 4))
            run(Round(0, B - 3))
            run(Round(0, B - 2, load=False))
            run(Round(0, B - 1, LAST_ROUND, more=False, load=False))

        def w_stage():
            flat = prob[:, :, :].rearrange("p a b -> p (a b)")[:, 0:C * (F1 + 2)]
            return flat.rearrange("p (c f) -> p c f", c=C)

        def rows_of(h):
            return slice(DH * (h % 2), DH * (h % 2) + DH), slice(DH - DH * (h % 2), 2 * DH - DH * (h % 2))

        block = ctx.enter_context(nc.Block())

        @block.sync
        def _(sp):
            def load_tokens(R, i):
                rows = x_rows[R.rows(2, i), :]
                if R.last:
                    sp.wait_ge(y_stored[i], R.n(16, 0))
                elif R.k == 0:
                    sp.wait_ge(w_lo, 4)
                sp.dma_start(tokens[R.buffer(2)][:, i, :], rows).then_inc(x_loaded[i], 16)

            def copy_head(R, pair, which):
                h = 2 * pair + which
                own, _ = rows_of(h)
                if which == 0:
                    sp.wait_ge(ring_done, R.ring(f"k{pair}", 1))
                elif due(R.n(32, 4 * (h - 1))):
                    sp.wait_ge(s_mm, R.n(32, 4 * (h - 1)))
                for half, rows in ((HI, slice(0, DH)), (LO, slice(DH, P))):
                    sp.dma_start(k_st[rows, h % 2, :, :].bitcast(F32),
                                 k_pair[own, :, :].bitcast(F32)).then_inc(head_copied[which], 16)
                    sp.dma_start(q_st[rows, h % 2, :].bitcast(F32),
                                 q_pair[own, half, :].bitcast(F32)).then_inc(head_copied[which], 16)

            def extra(R, names):
                for kind, i in R.pieces(names):
                    if kind == "cpA":
                        copy_head(R, i, 0)
                    if kind == "cpB":
                        copy_head(R, i, 1)
                    if kind == "fin":
                        rows = out_rows[R.rows(-1, i), :]
                        sp.wait_ge(y_ready, R.n(4, i - 3))
                        sp.dma_start(rows, tokens[R.buffer(-1)][:, i, :]).then_inc(y_stored[i], 16)
                    if kind == "ld":
                        load_tokens(R, i)

            def run_round(R):
                for steps in SP_PLAN:
                    extra(R, steps)

            sp.dma_start(w_stage()[:, :, 0:F1], W.rearrange("(c p) f -> p c f", p=P)).then_inc(w_loaded[0], 16)
            for j in range(2):
                sp.dma_start(alpha[:, j, 0:F1], a[j, :, 0].partition_broadcast(P)).then_inc(a_loaded, 16)
            for i in range(T):
                load_tokens(start, i)
            sp.dma_start(bo_wide[:, :], bo.partition_broadcast(P)).then_inc(small_loaded, 16)
            for dst, src in ((bq_col, bq), (bk_col, bk), (bv_col, bv)):
                sp.dma_start(dst[:, :], src).then_inc(small_loaded, 16)
            sp.dma_start(tokens[2][:, :, :].bitcast(I32), adj.rearrange("(t p) k -> p t k", p=P)).then_inc(adj_loaded, 16)
            for j, w in enumerate((WqT, WkT, WvT, WoT)):
                if j == 0:
                    sp.wait_ge(mask_built, 2)
                else:
                    sp.wait_ge(w_lo, j)
                stage = tokens[2] if j % 2 == 0 else prob
                sp.dma_start(stage[:, :, :], w.rearrange("(c p) n -> p c n", p=P)).then_inc(w_loaded[1 + j], 16)
                if j == 1:
                    for i in range(T):
                        load_tokens(prologue, i)
            extra(prologue, PROLOGUE)
            all_rounds(sp, run_round)
            extra(end, ENDING)
            for i in range(T):
                sp.wait_ge(y_stored[i], 16 * B)

        @block.tensor
        def _(pe):
            def ring(R, name):
                if due(R.ring(name, -1)):
                    pe.wait_ge(ring_done, R.ring(name, -1))
                return R_bank[R.bank(name)]

            def solo(R, name):
                before = solo_count(R, name, -1 if R.prologue else 0)
                if due(before):
                    pe.wait_ge(solo_done, before)
                return solo_bank(R, name)

            def solo_turn(bank, src):
                for c in range(4):
                    last = pe.transpose(bank[:, c * P:(c + 1) * P], src[:, c * P:(c + 1) * P], ident[:, :])
                last.then_inc(solo_mm, 1)

            def project(dst, stationary, moving, done, last_chunk=None):
                todo = [(c, s, m) for c in range(C) for s, m in PARTS]
                for c, s, m in todo:
                    if last_chunk is not None and (c, s, m) == todo[-len(PARTS)]:
                        pe.wait_ge(o_lo, last_chunk)
                    last = pe.matmul(dst, stationary(s, c), moving(m, c), start=(c, s, m) == todo[0],
                                     stop=(c, s, m) == todo[-1])
                last.then_inc(done, 1)

            def piece(R, kind, i):
                name = kind if kind == "N" else f"{kind}{i}"
                if kind == "A":
                    pe.wait_ge(x_loaded[i], R.n2(16, 16))
                    solo_turn(solo(R, name), tokens[R.buffer(2)][:, i, :])
                if kind == "B":
                    out_b = solo(R, name)
                    if R.prologue:
                        pe.wait_ge(solo_done, solo_count(R, f"A{i}"))
                    project(out_b[:, 0:F1 + 2], lambda s, c: turned[:, i % 2, s, c, :], lambda m, c: w0[:, m, c, :],
                            solo_mm)
                if kind == "N":
                    pe.wait_ge(nb_wide, R.nx(4, 4))
                    solo_turn(solo(R, "N"), n_wide[:, :])
                if kind == "C":
                    pe.wait_ge(a_exp, R.nx(4, i + 1))
                    solo_turn(solo(R, name), alpha[:, i % 2, :])
                if kind == "D":
                    out_b = ring(R, name)
                    pe.wait_ge(solo_done, solo_count(R, f"C{i}"))
                    project(out_b[:, 0:F1], lambda s, c: turned[:, i % 2, s, c, :], lambda m, c: h0[:, m, c, :],
                            ring_mm)
                if kind == "E":
                    pe.wait_ge(x1_ready, R.nx(4, i + 1))
                    solo_turn(solo(R, name), tokens[R.buffer(1)][:, i, :])
                if kind in ("q", "k"):
                    if name == "q4":
                        pe.wait_ge(solo_done, solo_count(R, "E3"))
                    c0, w = (i % 4) * P, wq if kind == "q" else wk
                    project(ring(R, name)[:, :], lambda s, c: w[:, s, c, c0:c0 + P], lambda m, c: x1T[:, m, c, :],
                            ring_mm)
                if kind in ("V", "W"):
                    if R.prologue and i == 0:
                        pe.wait_ge(w_lo, 4)
                    if kind == "V":
                        pe.wait_ge(solo_done, solo_count(R, f"E{i}"))
                    c0 = 0 if kind == "V" else D // 2
                    project(ring(R, name)[:, 0:D // 2], lambda s, c: x1T[:, s, c, i * P:(i + 1) * P],
                            lambda m, c: wv[:, m, c, c0:c0 + D // 2], ring_mm)
                if kind == "O":
                    out_b = ring(R, name)
                    if i == 0:
                        pe.wait_ge(o_lo, R.n(4, -1))
                    project(out_b[:, :], lambda s, c: oT[:, s, c, i * P:(i + 1) * P],
                            lambda m, c: wo[:, m, c, :], ring_mm, R.n(4, 0) if i == 0 else None)
                if kind == "pv":
                    weigh(R, -1, 1)

            def scores(R, h, t):
                if t == 0:
                    pe.wait_ge(head_copied[h % 2], R.n(256, 64 * (h // 2 + 1)))
                if due(R.n(32, 4 * h + t - 1)):
                    pe.wait_ge(s_red, R.n(32, 4 * h + t - 1))
                for part in (HI, LO):
                    last = pe.matmul(S_bank[t % 2][:, :], q_st[:, h % 2, t * P:(t + 1) * P],
                                     k_st[:, h % 2, part, :], start=part == HI, stop=part == LO)
                last.then_inc(s_mm, 1)

            def turn_probs(R, h, t):
                pe.wait_ge(p_norm, R.n(32, 4 * h + t + 1))
                if due(R.n(16, 2 * h + t // 2)):
                    pe.wait_ge(t_lo[t % 2], R.n(16, 2 * h + t // 2))
                for c in range(T):
                    last = pe.transpose(T_bank[t % 2][:, c * P:(c + 1) * P], prob[:, t, c * P:(c + 1) * P],
                                        ident[:, :])
                last.then_inc(t_mm, 1)

            def weigh(R, h, half):
                for b in range(2):
                    pe.wait_ge(t_lo[b], R.n(16, 2 * h + half + 1))
                if half == 0 and h == 0:
                    pe.wait_ge(ring_done, R.ring("k1", -1))
                if half == 0 and h == HEADS // 2:
                    pe.wait_ge(ring_done, R.ring("W3", 1))
                if half == 0 and due(R.n(8, h)):
                    pe.wait_ge(o_sum, R.n(8, h))
                todo = [(c, s) for c in range(T) for s in (HI, LO)]
                for c, s in todo:
                    last = pe.matmul(O_bank[:, half * 2 * P:(half + 1) * 2 * P], v_st[:, c, h % HEADS, :],
                                     probT[:, half, s, c, :], start=(c, s) == todo[0], stop=(c, s) == todo[-1])
                last.then_inc(pv_mm[half], 1)

            def run_round(R):
                for slot, steps in enumerate(TENSOR_PLAN):
                    h, t = slot // T, slot % T
                    for kind, i in R.pieces(steps):
                        if kind == "turn":
                            turn_probs(R, h, t)
                        elif kind == "scores":
                            if h < HEADS - 1 or R.more:
                                scores(R, h + 1, t)
                        elif kind == "weighA":
                            weigh(R, h, 0)
                        elif kind == "weighB":
                            weigh(R, h - 1, 1)
                        else:
                            piece(R, kind, i)

            pe.wait_ge(ident_built, IDENT)
            for kind, i in start.pieces(START):
                if (kind, i) == ("B", 0):
                    pe.wait_ge(w_lo, 1)
                piece(start, kind, i)
            for kind, i in prologue.pieces(PROLOGUE):
                piece(prologue, kind, i)
            pe.wait_ge(w_lo, 5)
            for t in range(T):
                scores(prologue, HEADS, t)
            all_rounds(pe, run_round)
            for kind, i in end.pieces(ENDING):
                piece(end, kind, i)

        @block.scalar
        def _(act):
            def split_hi(dst, src, done):
                act.activation(dst, src, ACT.Copy).then_inc(done, 1)

            def qk_of_pair_hi(R, pair):
                for which in range(2):
                    if due(R.n(256, 64 * pair)):
                        act.wait_ge(head_copied[which], R.n(256, 64 * pair))
                for kind, b_col, dst in (("q", bq_col, q_pair), ("k", bk_col, k_pair)):
                    ring_mm_value = R.ring("k1") if (kind, pair) == ("q", 1) else R.ring(f"{kind}{pair}", 1)
                    act.wait_ge(ring_mm, ring_mm_value)
                    act.activation(dst[:, HI, :], pair_bank(R, kind, pair)[:, :], ACT.Identity,
                                   bias=b_col[:, pair % 4:pair % 4 + 1]).then_inc(qk_hi, 1)

            def layer_apply(R, which, ahead, i, done):
                t_ap = tokens[R.buffer(ahead)][:, i, :]
                act.activation(t_ap, t_ap, ACT.Identity, bias=shift[which][:, i:i + 1],
                               scale=rstd[which][:, i:i + 1]).then_inc(done, 1)

            def piece(R, kind, i):
                name = kind if kind == "N" else f"{kind}{i}"
                if kind in ("A", "C"):
                    act.wait_ge(solo_mm, solo_count(R, name))
                    if name in ("A2", "A3"):
                        act.wait_ge(solo_mm, solo_count(R, f"B{i - 2}"))
                    if name in ("C2", "C3"):
                        act.wait_ge(ring_mm, R.ring(f"D{i - 2}", 1))
                    split_hi(turned[:, i % 2, HI, :, :], solo_bank(R, name)[:, :].rearrange("p (c t) -> p c t", c=C), solo_hi)
                if kind == "B":
                    act.wait_ge(solo_mm, solo_count(R, name))
                    split_hi(h0[:, HI, i, :], solo_bank(R, name)[:, 0:F1], solo_hi)
                if kind == "pre":
                    if i == 0:
                        act.wait_ge(solo_done, solo_count(R, "N"))
                    if i >= 2:
                        act.wait_ge(solo_mm, solo_count(R, f"C{i - 2}"))
                    act.activation(alpha[:, i % 2, :], n_wide[:, :], ACT.Identity,
                                   bias=terms[:, i, 0:1]).then_inc(a_pre, 1)
                if kind == "aexp":
                    act.wait_ge(a_red, R.nx(4, i + 1))
                    act.activation(alpha[:, i % 2, :], alpha[:, i % 2, :], ACT.Exp, bias=a_negmax[:, i:i + 1],
                                   scale=-1.0, accum_out=a_sum[:, i:i + 1]).then_inc(a_exp, 1)
                if kind == "lap":
                    act.wait_ge(ln_pool[0], R.nx(2, 2))
                    layer_apply(R, 0, 1, i, x1_ready)
                if kind == "E":
                    act.wait_ge(solo_mm, solo_count(R, name))
                    if i == 0 and not R.prologue:
                        act.wait_ge(ring_mm, R.ring("k3", 1))
                    split_hi(x1T[:, HI, :, i * P:(i + 1) * P], solo_bank(R, name)[:, :].rearrange("p (c t) -> p c t", c=C), solo_hi)
                if kind == "w":
                    act.wait_ge(w_loaded[1 + i], 16)
                    split_hi((wq, wk, wv, wo)[i][:, HI, :, :], (tokens[2], prob)[i % 2][:, :, :], w_hi)
                if kind == "evQ":
                    qk_of_pair_hi(R, i)
                if kind in ("evV", "evW"):
                    v, h0_ = kind[-1], 0 if kind == "evV" else HEADS // 2
                    act.wait_ge(ring_mm, R.ring(f"{v}{i}", 1))
                    if i == 0:
                        if due(R.n(8, h0_ or 0)) and not R.prologue:
                            act.wait_ge(pv_mm[1], R.n(8, 4) if kind == "evV" else R.n(8, 0))
                    split_hi(v_st[:, i, h0_:h0_ + HEADS // 2, 0:DH],
                             R_bank[R.bank(f"{v}{i}")][:, 0:D // 2].rearrange("p (h d) -> p h d", d=DH), v_hi)
                if kind == "pv":
                    head_lows(R, -1)
                    pair_hi(R, -1)
                if kind == "fin":
                    act.wait_ge(ln_pool[1], R.n(2, 0))
                    layer_apply(R, 1, -1, i, y_ready)

            def exps(R, h, t):
                act.wait_ge(s_red, R.n(32, 4 * h + t + 1))
                act.activation(prob[:, t, :], prob[:, t, :], ACT.Exp, bias=negmax[:, t:t + 1], scale=-1.0,
                               accum_out=psum_row[:, t:t + 1]).then_inc(p_exp, 1)

            def probs_hi(R, h, t):
                if due(R.n(8, h)):
                    act.wait_ge(pv_mm[t // 2], R.n(8, h))
                act.wait_ge(t_mm, R.n(32, 4 * h + t + 1))
                split_hi(probT[:, t // 2, HI, :, (t % 2) * P:(t % 2 + 1) * P],
                         T_bank[t % 2][:, :].rearrange("p (c q) -> p c q", c=T), t_hi)

            def head_lows(R, h):
                own, _ = rows_of(h)
                if due(R.n(4, h // 2)):
                    act.wait_ge(o_lo, R.n(4, h // 2))
                act.wait_ge(pv_mm[1], R.n(8, h + 1))
                act.activation(o_pair[own, :], O_bank[DH:2 * DH, :], ACT.Identity,
                               bias=bv_col[own, h // 2 % 4:h // 2 % 4 + 1]).then_inc(o_lows, 1)

            def pair_hi(R, pair):
                if pair == 0 and R.last:
                    act.wait_ge(ring_mm, R.ring("O3", 1))
                act.wait_ge(o_sum, R.n(8, 2 * pair + 2))
                split_hi(oT[:, HI, pair % 4, :], o_pair[:, :], o_hi)

            def run_round(R):
                for slot, steps in enumerate(SCALAR_PLAN):
                    h, t = slot // T, slot % T
                    for kind, i in R.pieces(steps):
                        if kind == "hi":
                            probs_hi(R, h, t)
                        elif kind == "exp":
                            if h < HEADS - 1 or R.more:
                                exps(R, h + 1, t)
                        elif kind == "lows":
                            head_lows(R, h - 1)
                        elif kind == "pair":
                            pair_hi(R, h // 2 - 1)
                        else:
                            piece(R, kind, i)

            act.wait_ge(w_loaded[0], 16)
            act.wait_ge(wa_done, 2 * C)
            split_hi(w0[:, HI, :, :], w_stage(), w_hi)
            act.wait_ge(small_loaded, SMALL)
            for R, pieces in ((start, START), (prologue, PROLOGUE)):
                for kind, i in R.pieces(pieces):
                    piece(R, kind, i)
            for t in range(T):
                exps(prologue, HEADS, t)
            all_rounds(act, run_round)
            for kind, i in end.pieces(ENDING):
                piece(end, kind, i)

        @block.vector
        def _(dve):
            def gate(i):
                dve.memset(gate_dve[:, i:i + 1], 0.0)

            def split_lo(dst, src, hi, done):
                dve.tensor_tensor(dst, src, hi.bitcast(F32), ALU.subtract).then_inc(done, 1)

            def layer_stats(which, count, i, t_ap):
                dve.bn_stats(stats[which][:, i, :], t_ap).then_inc(ln_dve[which], 1)
                dve.wait_ge(ln_dve[which], count(2 * i + 1))
                gate(which * T + i)
                dve.bn_aggr(meanvar[which][:, i, :], stats[which][:, i, :]).then_inc(ln_dve[which], 1)

            def layer_scales(which, count):
                dve.wait_ge(ln_dve[which], count(2 * T))
                dve.tensor_scalar(var_eps[which][:, :], meanvar[which][:, :, 1], EPS, None,
                                  ALU.add).then_inc(ln_dve[which], 1)
                dve.tensor_scalar(neg_mean[which][:, :], meanvar[which][:, :, 0], -1.0, None,
                                  ALU.mult).then_inc(ln_dve[which], 1)

            def qk_of_pair_lo(R, pair):
                for j, (kind, b_col, dst) in enumerate((("q", bq_col, q_pair), ("k", bk_col, k_pair))):
                    dve.wait_ge(qk_hi, R.n(8, 2 * pair + j + 1))
                    dve.scalar_tensor_tensor(out=dst[:, LO, :], in0=pair_bank(R, kind, pair)[:, :],
                                             scalar=b_col[:, pair % 4:pair % 4 + 1],
                                             in1=dst[:, HI, :].bitcast(F32), op0=ALU.add,
                                             op1=ALU.subtract).then_inc(ring_done, 1)

            def solo_hi_count(R, name):
                if R.prologue:
                    return len([u for u in FIRST_SOLO[:first_solo(R, name) + 1] if u != "N"])
                n = R.n2 if name[0] in "AB" else R.nx
                return n(len(SOLO) - 1, len([u for u in SOLO[:SOLO.index(name) + 1] if u != "N"]))

            def piece(R, kind, i):
                name = kind if kind == "N" else f"{kind}{i}"
                if kind in ("A", "C"):
                    if kind == "C":
                        dve.wait_ge(a_exp, R.nx(4, i + 1))
                        dve.reciprocal(a_rsum[:, i:i + 1], a_sum[:, i:i + 1]).then_inc(a_inv, 1)
                    dve.wait_ge(solo_hi, solo_hi_count(R, name))
                    split_lo(turned[:, i % 2, LO, :, :], solo_bank(R, name)[:, :].rearrange("p (c t) -> p c t", c=C),
                             turned[:, i % 2, HI, :, :], solo_done)
                if kind == "B":
                    dve.wait_ge(solo_hi, solo_hi_count(R, name))
                    split_lo(h0[:, LO, i, :], solo_bank(R, name)[:, 0:F1], h0[:, HI, i, :], h_lo)
                    dve.tensor_copy(terms[:, i, :], solo_bank(R, name)[:, F1:F1 + 2]).then_inc(terms_ready, 1)
                    t_ap = tokens[R.buffer(2)][:, i, F1:D]
                    dve.tensor_tensor(t_ap, solo_bank(R, name)[:, 0:F1], t_ap, ALU.add).then_inc(solo_done, 1)
                if kind == "N":
                    dve.wait_ge(solo_mm, solo_count(R, "N"))
                    dve.tensor_copy(n_wide[:, :], solo_bank(R, name)[:, :]).then_inc(solo_done, 1)
                if kind == "red":
                    al = alpha[:, i % 2, :]
                    dve.wait_ge(a_pre, R.nx(4, i + 1))
                    dve.scalar_tensor_tensor(out=al, in0=al, scalar=LEAK, in1=al, op0=ALU.mult,
                                             op1=ALU.max).then_inc(a_leaky, 1)
                    dve.wait_ge(a_leaky, R.nx(4, i + 1))
                    gate(2 * T + i)
                    dve.tensor_tensor_reduce(al, al, mask[:, i, :], -1.0, HUGE, ALU.add, ALU.min,
                                             a_negmax[:, i:i + 1]).then_inc(a_red, 1)
                if kind == "evD":
                    out_name, t_ap = f"D{i}", tokens[R.buffer(1)][:, i, 0:F1]
                    dve.wait_ge(a_inv, R.nx(4, i + 1))
                    dve.wait_ge(ring_mm, R.ring(out_name, 1))
                    dve.scalar_tensor_tensor(out=t_ap, in0=R_bank[R.bank(out_name)][:, 0:F1],
                                             scalar=a_rsum[:, i:i + 1], in1=t_ap, op0=ALU.mult,
                                             op1=ALU.add).then_inc(ring_done, 1)
                if kind == "lst":
                    dve.wait_ge(ring_done, R.ring(f"D{i}", 1))
                    layer_stats(0, lambda c: R.nx(10, c), i, tokens[R.buffer(1)][:, i, :])
                if kind == "lrs":
                    layer_scales(0, lambda c: R.nx(10, c))
                if kind == "E":
                    dve.wait_ge(solo_hi, solo_hi_count(R, name))
                    split_lo(x1T[:, LO, :, i * P:(i + 1) * P], solo_bank(R, name)[:, :].rearrange("p (c t) -> p c t", c=C),
                             x1T[:, HI, :, i * P:(i + 1) * P], solo_done)
                if kind == "w":
                    w = (wq, wk, wv, wo)[i]
                    dve.wait_ge(w_hi, 2 + i)
                    split_lo(w[:, LO, :, :], (tokens[2], prob)[i % 2][:, :, :], w[:, HI, :, :], w_lo)
                if kind == "evQ":
                    qk_of_pair_lo(R, i)
                if kind in ("evV", "evW"):
                    v, h0_ = kind[-1], 0 if kind == "evV" else HEADS // 2
                    dve.wait_ge(v_hi, R.n(8, 4 + i + 1) if kind == "evW" else R.nx(8, i + 1))
                    split_lo(v_st[:, i, h0_:h0_ + HEADS // 2, DH:2 * DH],
                             R_bank[R.bank(f"{v}{i}")][:, 0:D // 2].rearrange("p (h d) -> p h d", d=DH),
                             v_st[:, i, h0_:h0_ + HEADS // 2, 0:DH], ring_done)
                if kind == "pv":
                    head_sum(R, -1)
                if kind == "evO":
                    out_name, t_ap = f"O{i}", tokens[R.buffer(-1)][:, i, :]
                    dve.wait_ge(bo_added, R.n(4, i - 3))
                    dve.wait_ge(ring_mm, R.ring(out_name, 1))
                    dve.tensor_tensor(t_ap, R_bank[R.bank(out_name)][:, :], t_ap, ALU.add).then_inc(ring_done, 1)
                if kind == "yst":
                    dve.wait_ge(ring_done, R.ring(f"O{i}", 1))
                    layer_stats(1, lambda c: R.n(10, c - 10), i, tokens[R.buffer(-1)][:, i, :])
                if kind == "yrs":
                    layer_scales(1, lambda c: R.n(10, c - 10))

            def reduce_scores(R, h, t, unit_before=None):
                if due(R.n(32, 4 * (h - 1) + t + 1)) and not R.prologue:
                    dve.wait_ge(t_mm, R.n(32, 4 * (h - 1) + t + 1))
                dve.wait_ge(s_mm, R.n(32, 4 * h + t + 1))
                if unit_before is not None:
                    invert_sums(R, *unit_before)
                dve.tensor_tensor_reduce(prob[:, t, :], S_bank[t % 2][:, :], mask[:, t, :], -SCALE, HUGE, ALU.add,
                                         ALU.min, negmax[:, t:t + 1]).then_inc(s_red, 1)

            def invert_sums(R, h, t):
                dve.wait_ge(p_exp, R.n(32, 4 * h + t + 1))
                dve.reciprocal(rsum[:, t:t + 1], psum_row[:, t:t + 1]).then_inc(p_inv, 1)

            def probs_lo(R, h, t):
                dve.wait_ge(t_hi, R.n(32, 4 * h + t + 1))
                cols = slice((t % 2) * P, (t % 2 + 1) * P)
                split_lo(probT[:, t // 2, LO, :, cols], T_bank[t % 2][:, :].rearrange("p (c q) -> p c q", c=T),
                         probT[:, t // 2, HI, :, cols], t_lo[t % 2])

            def head_sum(R, h):
                own, _ = rows_of(h)
                dve.wait_ge(o_lows, R.n(8, h + 1))
                dve.tensor_tensor(o_pair[own, :], O_bank[0:DH, :], o_pair[own, :], ALU.add).then_inc(o_sum, 1)

            def run_round(R):
                for slot, steps in enumerate(VECTOR_PLAN):
                    h, t = slot // T, slot % T
                    for kind, i in R.pieces(steps):
                        if kind == "lo":
                            probs_lo(R, h, t)
                        elif kind == "reduce":
                            before = (h + 1, t - 1) if t > 0 else (h, T - 1) if h > 0 or R.last else None
                            if h < HEADS - 1 or R.more:
                                reduce_scores(R, h + 1, t, before)
                            elif t == 0:
                                invert_sums(R, *before)
                        elif kind == "sum":
                            head_sum(R, h - 1)
                        else:
                            piece(R, kind, i)

            dve.memset(minus_half[:, :], -0.5).then_inc(mask_built, 1)
            dve.wait_ge(w_loaded[0], 16)
            dve.wait_ge(a_loaded, 2 * 16)
            for j in range(2):
                for c in range(C):
                    if j + c > 0:
                        dve.wait_ge(wa_done, j * C + c)
                    dve.tensor_tensor_reduce(n_wide[:, 0:F1], w_stage()[:, c, 0:F1], alpha[:, j, 0:F1], 1.0, 0.0,
                                             ALU.mult, ALU.add, w_stage()[:, c, F1 + j:F1 + j + 1]).then_inc(wa_done, 1)
            dve.wait_ge(w_hi, 1)
            split_lo(w0[:, LO, :, :], w_stage(), w0[:, HI, :, :], w_lo)
            dve.wait_ge(adj_loaded, 16)
            dve.tensor_scalar(mask[:, :, :], tokens[2][:, :, :].bitcast(I32), 0.0, MASKED, ALU.is_equal,
                              ALU.mult).then_inc(mask_built, 1)
            dve.wait_ge(small_loaded, SMALL)
            for R, pieces in ((start, START), (prologue, PROLOGUE)):
                for kind, i in R.pieces(pieces):
                    piece(R, kind, i)
            for t in range(T):
                reduce_scores(prologue, HEADS, t)
                invert_sums(prologue, HEADS, t)
            all_rounds(dve, run_round)
            for kind, i in end.pieces(ENDING):
                piece(end, kind, i)

        @block.gpsimd
        def _(pool):
            def normalise(R, h, t):
                pool.wait_ge(p_inv, R.n(32, 4 * h + t + 1))
                pool.tensor_tensor(prob[:, t, :], prob[:, t, :], rsum[:, t:t + 1].to_broadcast([P, N]),
                                   ALU.mult).then_inc(p_norm, 1)

            def scales(which, full, half):
                pool.wait_ge(ln_dve[which], full)
                pool.tensor_tensor(rstd[which][:, :], var_eps[which][:, :], minus_half[:, :],
                                   ALU.pow).then_inc(ln_pool[which], 1)
                pool.wait_ge(ln_pool[which], half)
                pool.tensor_tensor(shift[which][:, :], neg_mean[which][:, :], rstd[which][:, :],
                                   ALU.mult).then_inc(ln_pool[which], 1)

            def pair_lo(R, pair):
                pool.wait_ge(o_hi, R.n(4, pair + 1))
                pool.tensor_tensor(oT[:, LO, pair % 4, :], o_pair[:, :], oT[:, HI, pair % 4, :].bitcast(F32),
                                   ALU.subtract).then_inc(o_lo, 1)

            def piece(R, kind, i):
                if kind == "nbm":
                    pool.wait_ge(terms_ready, R.n2(4, 4))
                    for j in range(T):
                        pool.tensor_tensor(n_wide[:, j * P:(j + 1) * P], terms[:, j, 1:2].to_broadcast([P, P]),
                                           zero[:, :].to_broadcast([P, P]), ALU.add).then_inc(nb_wide, 1)
                if kind == "lrs":
                    scales(0, R.nx(10, 10), R.nx(2, 1))
                if kind == "yrs":
                    scales(1, R.n(10, 0), R.n(2, -1))
                if kind == "bo":
                    pool.wait_ge(solo_mm, solo_count(R, f"E{i}"))
                    t_ap = tokens[R.buffer(1)][:, i, :]
                    pool.tensor_tensor(t_ap, t_ap, bo_wide[:, :], ALU.add).then_inc(bo_added, 1)
                if kind == "pv":
                    pair_lo(R, -1)

            def run_round(R):
                for slot, steps in enumerate(GPSIMD_PLAN):
                    h, t = slot // T, slot % T
                    for kind, i in R.pieces(steps):
                        if kind == "norm":
                            if t > 0 and (h < HEADS - 1 or R.more):
                                normalise(R, h + 1, t - 1)
                            if t == 0 and (h > 0 or R.last):
                                normalise(R, h, T - 1)
                        elif kind == "pair":
                            pair_lo(R, h // 2 - 1)
                        else:
                            piece(R, kind, i)

            pool.memset(zero[:, :], 0.0).then_inc(ident_built, 1)
            pool.memset(ident[:, :], 0.0).then_inc(ident_built, 1)
            pool.wait_ge(ident_built, 2)
            pool.affine_select(out=ident[:, :], in_=ident[:, :], compare_op=ALU.not_equal, fill=1.0, base=0,
                               pattern=[[-1, P]], channel_multiplier=1).then_inc(ident_built, 1)
            pool.wait_ge(small_loaded, SMALL)
            pool.wait_ge(mask_built, 1)
            for R, pieces in ((start, START), (prologue, PROLOGUE)):
                for kind, i in R.pieces(pieces):
                    piece(R, kind, i)
            for t in range(T):
                normalise(prologue, HEADS, t)
            all_rounds(pool, run_round)
            for kind, i in end.pieces(ENDING):
                piece(end, kind, i)


def kernel(x, adj, L0_gnn_W, L0_gnn_a, L1_gnn_Wq, L1_gnn_bq, L1_gnn_Wk, L1_gnn_bk, L1_gnn_Wv, L1_gnn_bv,
           L1_gnn_Wo, L1_gnn_bo):
    import numpy as np
    import concourse.bacc as bacc
    from concourse.bass_utils import run_bass_kernel_spmd

    def columns(b):
        return np.ascontiguousarray(np.asarray(b).reshape(-1, P).T)

    def turned(w):
        return np.ascontiguousarray(np.asarray(w).T)

    arrays = {
        "x": np.ascontiguousarray(x), "adj": np.ascontiguousarray(adj), "W": np.ascontiguousarray(L0_gnn_W),
        "a": np.ascontiguousarray(L0_gnn_a), "WqT": turned(L1_gnn_Wq), "bq": columns(L1_gnn_bq),
        "WkT": turned(L1_gnn_Wk), "bk": columns(L1_gnn_bk), "WvT": turned(L1_gnn_Wv), "bv": columns(L1_gnn_bv),
        "WoT": turned(L1_gnn_Wo), "bo": np.ascontiguousarray(L1_gnn_bo),
    }
    nc = bacc.Bacc("TRN2", target_bir_lowering=False, num_devices=1, dynamic_dma_scratch_size=1024)
    args = [nc.dram_tensor(name, v.shape, mybir.dt.from_np(v.dtype), kind="ExternalInput").ap()
            for name, v in arrays.items()]
    out = nc.dram_tensor("out", arrays["x"].shape, F32, kind="ExternalOutput").ap()
    graph_layers(nc, *args, out)
    r = run_bass_kernel_spmd(nc, [arrays], core_ids=[0])
    return r.results[0]["out"]
```
